# Optimizing a Trainium2 kernel written in Bass

```python
import numpy as np
import jax
import jax.numpy as jnp

def _softmax(x, axis=-1):
    return jax.nn.softmax(x, axis=axis)

def _gelu(x):
    return jax.nn.gelu(x, approximate=True)

def _silu(x):
    return jax.nn.silu(x)

def _sigmoid(x):
    return jax.nn.sigmoid(x)

def _layernorm(x, axis=-1, eps=1e-05):
    m = jnp.mean(x, axis=axis, keepdims=True)
    v = jnp.var(x, axis=axis, keepdims=True)
    return (x - m) / jnp.sqrt(v + eps)

def _scatter_add(tgt, idx, src, axis=0):
    return tgt.at[idx].add(src)

def _segment_sum(src, seg, n):
    return jax.ops.segment_sum(src, seg, n)
kernel_name = 'mk_adj_resnorm_d2_adj_r2_2e016f'

def setup_inputs(seed: int=0):
    np.random.seed(seed)
    _w = jnp.asarray

    def _rec_inputs():
        import jax
        import jax.numpy as jnp
        _gk = jax.random.key(seed)
        x = -0.0005207 + 1.001 * jax.random.normal(jax.random.fold_in(_gk, 1), (4096, 128), jnp.float32)
        _w = (1.0 + jnp.arange(4096, dtype=jnp.float32)) ** (-0.5)
        _w = _w / _w.mean()
        _pij = jnp.clip(0.00195312 * _w[:, None] * _w[None, :], 0.0, 1.0)
        _a = jax.random.uniform(jax.random.fold_in(_gk, 2), (4096, 4096)) < _pij
        _a = jnp.logical_or(_a, jnp.eye(4096, dtype=bool))
        _af = _a.astype(jnp.float32)
        _af = _af * jax.random.uniform(jax.random.fold_in(_gk, 3), (4096, 4096), jnp.float32, 0.05, 1)
        adj = _af
        return (x, adj)
    x, adj = _rec_inputs()

    def _L0_gnn_setup():
        import jax, jax.numpy as jnp
        import numpy as np
        N = 4096
        D = 128
        L = 3

        def _cxin_conv(x, a, eps, W, b):
            ax = a @ x
            h = ax + (1.0 + eps[0]) * ax
            for i in range(L):
                h = jax.nn.relu(h @ W[i].T + b[i])
            return h
        key = jax.random.key(seed)
        ks = jax.random.split(key, 8)
        s = 1.0 / np.sqrt(D)
        return {'x1': jax.random.normal(ks[0], (N, D), jnp.float32), 'x2': jax.random.normal(ks[1], (N, D), jnp.float32), 'G1': jax.random.uniform(ks[2], (N, N), jnp.float32), 'G2': jax.random.uniform(ks[3], (N, N), jnp.float32), 'eps1': jnp.zeros((1,), jnp.float32), 'eps2': jnp.zeros((1,), jnp.float32), 'W1': jax.random.normal(ks[4], (L, D, D), jnp.float32) * s, 'b1': jnp.zeros((L, D), jnp.float32), 'W2': jax.random.normal(ks[5], (L, D, D), jnp.float32) * s, 'b2': jnp.zeros((L, D), jnp.float32), 'Wm': jax.random.normal(ks[6], (D, 2 * D), jnp.float32) * (1.0 / np.sqrt(2 * D)), 'bm': jnp.zeros((D,), jnp.float32)}
    _L0_gnn_all = _L0_gnn_setup()
    _L0_gnn_in = {k: v for k, v in _L0_gnn_all.items() if k in ('x2', 'eps1', 'eps2', 'W1', 'b1', 'W2', 'b2', 'Wm', 'bm')}
    del _L0_gnn_all

    def _L1_gnn_setup():
        import jax, jax.numpy as jnp
        import numpy as np
        N = 4096
        F_IN = 128
        F_OUT = 128
        key = jax.random.key(seed)
        k1, k2, k3 = jax.random.split(key, 3)
        H = jax.random.normal(k1, (N, F_IN), dtype=jnp.float32)
        A_tilde = jax.random.uniform(k2, (N, N), dtype=jnp.float32)
        limit = np.sqrt(6.0 / (F_IN + F_OUT)).astype(np.float32)
        W = jax.random.uniform(k3, (F_IN, F_OUT), dtype=jnp.float32, minval=-limit, maxval=limit)
        return {'H': H, 'A_tilde': A_tilde, 'W': W}
    _L1_gnn_all = _L1_gnn_setup()
    _L1_gnn_in = {k: v for k, v in _L1_gnn_all.items() if k in ('W',)}
    del _L1_gnn_all
    return {'x': x, 'adj': adj, 'L0_gnn_x2': _L0_gnn_in['x2'], 'L0_gnn_eps1': _L0_gnn_in['eps1'], 'L0_gnn_eps2': _L0_gnn_in['eps2'], 'L0_gnn_W1': _L0_gnn_in['W1'], 'L0_gnn_b1': _L0_gnn_in['b1'], 'L0_gnn_W2': _L0_gnn_in['W2'], 'L0_gnn_b2': _L0_gnn_in['b2'], 'L0_gnn_Wm': _L0_gnn_in['Wm'], 'L0_gnn_bm': _L0_gnn_in['bm'], 'L1_gnn_W': _L1_gnn_in['W']}

def reference(x, adj, L0_gnn_x2, L0_gnn_eps1, L0_gnn_eps2, L0_gnn_W1, L0_gnn_b1, L0_gnn_W2, L0_gnn_b2, L0_gnn_Wm, L0_gnn_bm, L1_gnn_W):
    import jax
    import jax.numpy as jnp

    def _L0_gnn_ref(x1, x2, G1, G2, eps1, eps2, W1, b1, W2, b2, Wm, bm):
        import jax, jax.numpy as jnp
        import numpy as np
        N = 4096
        D = 128
        L = 3

        def _cxin_conv(x, a, eps, W, b):
            ax = a @ x
            h = ax + (1.0 + eps[0]) * ax
            for i in range(L):
                h = jax.nn.relu(h @ W[i].T + b[i])
            return h
        out1 = _cxin_conv(x1, G1, eps1, W1, b1)
        out2 = _cxin_conv(x2, G2, eps2, W2, b2)
        merged = jnp.concatenate((out1, out2), axis=1)
        return merged @ Wm.T + bm

    def _L1_gnn_ref(H, A_tilde, W):
        import jax, jax.numpy as jnp
        import numpy as np
        N = 4096
        F_IN = 128
        F_OUT = 128
        d_inv_sqrt = jnp.sum(A_tilde, axis=1) ** (-0.5)
        A_norm = d_inv_sqrt[:, None] * A_tilde * d_inv_sqrt[None, :]
        H_next = A_norm @ H @ W
        return jax.nn.relu(H_next)
    x = _layernorm(x + _L0_gnn_ref(x, L0_gnn_x2, adj, adj, L0_gnn_eps1, L0_gnn_eps2, L0_gnn_W1, L0_gnn_b1, L0_gnn_W2, L0_gnn_b2, L0_gnn_Wm, L0_gnn_bm), axis=-1)
    x = _layernorm(x + _L1_gnn_ref(x, adj, L1_gnn_W), axis=-1)
    return x

_drawn_inputs = setup_inputs


def setup_inputs(seed=0):
    import zlib

    import numpy as np

    out = dict(_drawn_inputs(seed))
    spreads = {'L0_gnn_b1': (0.0, 0.1), 'L0_gnn_b2': (0.0, 0.1), 'L0_gnn_bm': (0.0, 0.1)}
    factors = {}
    for name, (base, spread) in spreads.items():
        noise = np.random.default_rng([zlib.crc32(name.encode()), seed]).standard_normal(out[name].shape)
        drawn = base * np.exp(spread * noise) if base else spread * noise
        out[name] = jnp.asarray(drawn.astype(out[name].dtype))
    for name, factor in factors.items():
        out[name] = (out[name] * factor).astype(out[name].dtype)
    return out
```

```python
import concourse.bass as bass
from concourse import mybir

F32 = mybir.dt.float32
F32R = mybir.dt.float32r
ALU = mybir.AluOpType
ACT = mybir.ActivationFunctionType

P = 128
N = 4096
D = 128
BLOCK = 512
NB = N // BLOCK
JT = BLOCK // P
UT = 2
UNIT = UT * BLOCK
UPC = JT // UT
UPB = NB * UPC
LAYERS = 3
LN_EPS = 1e-5

EARLY = 2
ORDER = list(range(NB - 1, NB - 1 - EARLY, -1)) + list(range(NB - EARLY))
POS = {b: k for k, b in enumerate(ORDER)}
HB = NB - EARLY

RAW_SLOTS = 8
SPLIT_SLOTS = 4

SWEEP2 = [(i, [b for b in range(min(i, HB), NB)]) for i in range(NB)]
UNITS2 = [(i, b, u) for i, blocks in SWEEP2 for b in blocks for u in range(UPC)]
N1 = NB * UPB
FIRST = [min(m for m, x in enumerate(UNITS2) if x[0] == i) for i in range(NB)]
LAST = [max(m for m, x in enumerate(UNITS2) if x[0] == i) for i in range(NB)]
AGG_LAG, OUT_LAG, RELU_LAG, STATS_LAG, NORM_LAG = 4, 4, 8, 8, 9
STEPS2 = len(UNITS2) + NORM_LAG

W_LAYER = [[(3 * br + l) * D for l in range(LAYERS)] for br in range(2)]
W_MERGE = [6 * D, 7 * D]
W_GCN = 8 * D
B_LAYER = [[3 * br + l for l in range(LAYERS)] for br in range(2)]

TURNS = (NB - 2) // 2
HID_STEPS = 2 * (LAYERS + 1)
MLP_STEPS = 2 * LAYERS


def build(nc, adj, x1, x2, weights, biases, eps, bm, out):
    from contextlib import ExitStack

    with ExitStack() as ctx:
        def sb(name, shape, dt=F32):
            return ctx.enter_context(nc.sbuf_tensor(name, shape, dt))

        def bank(name):
            return ctx.enter_context(nc.psum_tensor(name, [P, BLOCK], F32))

        def sem(name):
            return ctx.enter_context(nc.semaphore(name))

        x_hi = [sb(f"x{br}_hi", [P, NB * BLOCK], F32R) for br in range(2)]
        x_lo = [sb(f"x{br}_lo", [P, NB * BLOCK], F32R) for br in range(2)]
        hs_hi = sb("hs_hi", [P, NB * BLOCK], F32R)
        hs_lo = sb("hs_lo", [P, NB * BLOCK], F32R)
        res = sb("res", [P, NB * BLOCK])
        part = sb("part", [P, NB * BLOCK])
        raw = sb("raw", [P, RAW_SLOTS * UNIT])
        a_hi = sb("a_hi", [P, SPLIT_SLOTS * UNIT], F32R)
        a_lo = sb("a_lo", [P, SPLIT_SLOTS * UNIT], F32R)
        rowacc = sb("rowacc", [P, UNIT])
        rowsum = sb("rowsum", [P, BLOCK])
        hid = [sb(f"hid{br}", [P, BLOCK]) for br in range(2)]
        wts = sb("wts", [P, 9 * D])
        bias = sb("bias", [P, 6])
        gain = sb("gain", [P, 2])
        bm_all = sb("bm_all", [P, D])
        ones = sb("ones", [P, 1])
        dinv = sb("dinv", [P, NB * JT])
        stats = sb("stats", [P, JT * 6])
        meanvar = sb("meanvar", [P, JT * 2])
        rstd = sb("rstd", [P, JT])
        root = sb("root", [P, 3 * JT])
        dcur = sb("dcur", [P, JT])

        sum_bank = [[bank(f"sum{par}{br}") for br in range(2)] for par in range(2)]
        ah_bank = bank("ah")
        mlp_bank = [bank(f"mlp{br}") for br in range(2)]
        mix_bank = bank("mix")
        ah2_bank = [sum_bank[0][0], ah_bank]
        z_bank = [sum_bank[0][1], sum_bank[1][1]]

        s_x = [sem(f"x_loaded{k}") for k in range(NB)]
        s_xh = [sem(f"x_hi_loaded{k}") for k in range(NB)]
        s_xp = sem("x_parts_ready")
        s_res = sem("x_plus_bm")
        s_w = sem("weights_loaded")
        s_ones = sem("ones_ready")
        s_gain = sem("gain_ready")
        s_raw = [sem(f"raw_loaded{s}") for s in range(RAW_SLOTS)]
        s_hi = sem("a_hi_ready")
        s_lo = sem("a_lo_ready")
        s_used = sem("split_slots_free")
        s_acc = sem("rowacc_step")
        s_hid = sem("hidden_ready")
        s_mlp = sem("layer_done")
        s_deg = sem("degree_done")
        s_dinv = sem("dinv_ready")
        s_mix = sem("mix_done")
        s_ln = sem("ln_step")
        s_h = sem("h_ready")
        s_part = sem("part_saved")
        s_agg = sem("agg_ready")
        s_z = sem("z_done")
        s_relu = sem("relu_ready")
        s_ln2 = sem("ln2_step")
        s_root = sem("root_step")
        s_tick = sem("vector_tick")
        s_sqrt = sem("sqrt_done")
        s_fin = sem("result_ready")
        s_out = sem("last_stored")
        s_out_pool = sem("others_stored")

        block = ctx.enter_context(nc.Block())

        LN_STEPS = 6
        LN2_STEPS = 4
        ROOT_STEPS = 4

        def slot(n):
            return raw[:, (n % RAW_SLOTS) * UNIT:(n % RAW_SLOTS + 1) * UNIT]

        def split(t, n):
            return t[:, (n % SPLIT_SLOTS) * UNIT:(n % SPLIT_SLOTS + 1) * UNIT]

        def cols(t, b, n=1):
            return t[:, b * BLOCK:(b + n) * BLOCK]

        def stage(k):
            return cols(part, k)

        @block.sync
        def _(sp):
            def load_x(k):
                sp.dma_start(cols(res, ORDER[k]), x1[ORDER[k]]).then_inc(s_x[k], 16)
                sp.dma_start(stage(k), x2[ORDER[k]]).then_inc(s_x[k], 16)

            load_x(0)
            for n in range(UPB):
                if n >= RAW_SLOTS:
                    sp.wait_ge(s_lo, n - RAW_SLOTS + 1)
                sp.dma_start(slot(n), adj[n]).then_inc(s_raw[n % RAW_SLOTS], 16)
                if n % UPC == UPC - 1 and n // UPC + 1 < NB:
                    load_x(n // UPC + 1)
            with sp.Fori(UPB // RAW_SLOTS, N1 // RAW_SLOTS) as turn:
                for s in range(RAW_SLOTS):
                    n = turn * RAW_SLOTS + s
                    sp.wait_ge(s_lo, turn * RAW_SLOTS + (s - RAW_SLOTS + 1))
                    sp.dma_start(slot(s), adj[bass.ds(n, 1)].rearrange("a p f -> p (a f)"))\
                      .then_inc(s_raw[s], 16)
            for m, (i, b, u) in enumerate(UNITS2):
                n = N1 + m
                sp.wait_ge(s_lo, n - RAW_SLOTS + 1)
                sp.dma_start(slot(n), adj[i * UPB + POS[b] * UPC + u]).then_inc(s_raw[n % RAW_SLOTS], 16)
            sp.wait_ge(s_fin, NB)
            sp.dma_start(out[NB - 1], cols(res, NB - 1)).then_inc(s_out, 16)
            sp.wait_ge(s_out, 16)

        @block.gpsimd
        def _(pool):
            pool.memset(ones[:, :], 1.0).then_inc(s_ones, 1)

            def load_hi(k):
                pool.dma_start(cols(x_hi[0], ORDER[k]), x1[ORDER[k]]).then_inc(s_xh[k], 16)
                pool.dma_start(cols(x_hi[1], ORDER[k]), x2[ORDER[k]]).then_inc(s_xh[k], 16)

            load_hi(0)
            load_hi(1)
            for k, b in enumerate(ORDER):
                if k + 2 < NB:
                    load_hi(k + 2)
                pool.wait_ge(s_x[k], 32)
                pool.wait_ge(s_xh[k], 32)
                pool.tensor_tensor(cols(x_lo[0], b), cols(res, b), cols(x_hi[0], b).bitcast(F32),
                                   ALU.subtract).then_inc(s_xp, 1)
                pool.tensor_tensor(cols(x_lo[1], b), stage(k), cols(x_hi[1], b).bitcast(F32),
                                   ALU.subtract).then_inc(s_xp, 1)
                pool.wait_ge(s_w, 64)
                pool.wait_ge(s_xp, 2 * k + 1)
                r = cols(res, b).rearrange("p (t d) -> p t d", d=D)
                pool.tensor_tensor(r, r, bm_all[:, None, :].to_broadcast([P, JT, D]),
                                   ALU.add).then_inc(s_res, 1)



            for i in range(NB - 1):
                pool.wait_ge(s_fin, i + 1)
                pool.dma_start(out[i], cols(res, i)).then_inc(s_out_pool, 16)
            pool.wait_ge(s_out_pool, 16 * (NB - 1))

        @block.scalar
        def _(act):
            act.dma_start(wts[:, :], weights).then_inc(s_w, 16)
            act.dma_start(bias[:, :], biases).then_inc(s_w, 16)
            act.dma_start(bm_all[:, :], bm.to_broadcast([P, D])).then_inc(s_w, 16)
            act.dma_start(gain[:, :], eps.to_broadcast([P, 2])).then_inc(s_w, 16)

            def high(n, s, loads):
                act.wait_ge(s_raw[s % RAW_SLOTS], loads)
                act.wait_ge(s_used, n + 1)
                nc.scalar.activation(split(a_hi, s), slot(s), ACT.Copy).then_inc(s_hi, 1)

            def sums_out(m, par):
                act.wait_ge(s_used, (m + 1) * UPB + SPLIT_SLOTS)
                for br in range(2):
                    nc.scalar.activation(hid[br][:, :], sum_bank[par][br][:, :], ACT.Identity,
                                         scale=gain[:, br:br + 1]).then_inc(s_hid, 1)

            def relus(m, l):
                for br in range(2):
                    act.wait_ge(s_mlp, m * MLP_STEPS + (2 * l + br + 1))
                    c = B_LAYER[br][l]
                    nc.scalar.activation(hid[br][:, :], mlp_bank[br][:, :], ACT.Relu,
                                         bias=bias[:, c:c + 1]).then_inc(s_hid, 1)

            def save_part(m):
                nc.scalar.activation(part[:, bass.ds(m * BLOCK, BLOCK)], ah_bank[:, :],
                                     ACT.Copy).then_inc(s_part, 1)

            def block_turn(g, par, has_part=lambda step: step()):
                for u in range(UPB):
                    high(g * UPB + u, u, g * (16 * UPB // RAW_SLOTS) + 16 * (u // RAW_SLOTS + 1))
                    if isinstance(g, int) and g == 0:
                        continue
                    if u == 2:
                        sums_out(g - 1, 1 - par)
                    if u == 3:
                        relus(g - 1, 0)
                        square_root((g - 1) * 2)
                    if u == 4:
                        relus(g - 1, 1)
                        relus(g - 1, 2)
                        has_part(lambda: save_part(g - 1))
                    if u == 6:
                        square_root((g - 1) * 2 + 1)

            def square_root(call):
                act.wait_ge(s_root, call * ROOT_STEPS + 1)
                nc.scalar.activation(root[:, JT:2 * JT], root[:, 0:JT], ACT.Sqrt).then_inc(s_sqrt, 1)

            def not_first(step):
                with act.If(turn > 0):
                    step()

            act.sem_inc(s_part, 1)
            act.wait_ge(s_gain, 1)
            block_turn(0, 0)
            with act.Fori(0, TURNS) as turn:
                block_turn(turn * 2 + 1, 1, not_first)
                block_turn(turn * 2 + 2, 0)
            block_turn(NB - 1, 1)
            for m in range(STEPS2):
                if m < len(UNITS2):
                    high(N1 + m, N1 + m, 16 * ((N1 + m) // RAW_SLOTS + 1))
                if m == 2:
                    sums_out(NB - 1, 1)
                    save_part(NB - 1)
                if m == 3:
                    relus(NB - 1, 0)
                    square_root((NB - 1) * 2)
                if m == 4:
                    relus(NB - 1, 1)
                    relus(NB - 1, 2)
                if m == 6:
                    square_root((NB - 1) * 2 + 1)
                for i in range(NB):
                    if LAST[i] + RELU_LAG == m:
                        act.wait_ge(s_z, i + 1)
                        if i >= 2:
                            act.wait_ge(s_ln2, LN2_STEPS * (i - 2) + 1)
                        for t in range(JT):
                            o = (i % 2) * BLOCK + t * P
                            c = i * JT + t
                            ins = nc.scalar.activation(rowacc[:, o:o + D], z_bank[i % 2][:, t * D:(t + 1) * D],
                                                       ACT.Relu, scale=dinv[:, c:c + 1])
                        ins.then_inc(s_relu, 1)
                    if LAST[i] + NORM_LAG == m:
                        square_root(2 * NB + i)

        @block.vector
        def _(dve):
            dve.wait_ge(s_w, 64)
            nc.vector.tensor_scalar(gain[:, :], gain[:, :], 1.0, 1.0, ALU.add, ALU.add).then_inc(s_gain, 1)

            def low(n, s):
                dve.wait_ge(s_hi, n + 1)
                nc.vector.tensor_tensor(split(a_lo, s), slot(s), split(a_hi, s).bitcast(F32),
                                        ALU.subtract).then_inc(s_lo, 1)

            value, sroot, fix = root[:, 0:JT], root[:, JT:2 * JT], root[:, 2 * JT:3 * JT]

            def inverse_root(call, r, done):
                base = call * ROOT_STEPS + 1
                dve.wait_ge(s_sqrt, call + 1)
                nc.vector.reciprocal(r, sroot).then_inc(s_root, 1)
                dve.wait_ge(s_root, base + 1)
                nc.vector.tensor_tensor(fix, r, r, ALU.mult).then_inc(s_root, 1)
                dve.wait_ge(s_root, base + 2)
                nc.vector.scalar_tensor_tensor(out=fix, in0=fix, scalar=-0.5, in1=value,
                                               op0=ALU.mult, op1=ALU.mult).then_inc(s_root, 1)
                dve.wait_ge(s_root, base + 3)
                nc.vector.scalar_tensor_tensor(out=r, in0=fix, scalar=1.5, in1=r,
                                               op0=ALU.add, op1=ALU.mult).then_inc(done, 1)

            def degree_value(m):
                dve.wait_ge(s_deg, m + 1)
                nc.vector.tensor_copy(value, mix_bank[:, 0:JT]).then_inc(s_root, 1)

            def degree(m):
                inverse_root(m * 2, dcur[:, :], s_dinv)
                dve.wait_ge(s_dinv, 2 * m + 1)
                nc.vector.tensor_copy(dinv[:, bass.ds(m * JT, JT)], dcur[:, :]).then_inc(s_dinv, 1)

            def statistics(r, s, base):
                for t in range(JT):
                    ins = nc.vector.bn_stats(stats[:, 6 * t:6 * t + 6], r(t))
                ins.then_inc(s, 1)
                dve.wait_ge(s, base + 1)
                dve.sem_inc(s_tick)
                for t in range(JT):
                    ins = nc.vector.bn_aggr(meanvar[:, 2 * t:2 * t + 2], stats[:, 6 * t:6 * t + 6])
                ins.then_inc(s, 1)
                dve.wait_ge(s, base + 2)
                nc.vector.tensor_scalar(value, meanvar[:, 1:2 * JT:2], LN_EPS, None, ALU.add)\
                  .then_inc(s_root, 1)

            def normalise(call, r, s, base, done):
                inverse_root(call, rstd[:, :], s)
                dve.wait_ge(s, base + 3)
                for t in range(JT):
                    ins = nc.vector.tensor_scalar(r(t), r(t), meanvar[:, 2 * t:2 * t + 1],
                                                  rstd[:, t:t + 1], ALU.subtract, ALU.mult)
                ins.then_inc(done, 1)

            def make_h(m):
                dve.wait_ge(s_mix, m + 1)
                dve.wait_ge(s_res, NB)
                b0 = m * BLOCK
                base = m * LN_STEPS
                nc.vector.tensor_tensor(res[:, bass.ds(b0, BLOCK)], mix_bank[:, :],
                                        res[:, bass.ds(b0, BLOCK)], ALU.add).then_inc(s_ln, 1)
                dve.wait_ge(s_ln, base + 1)
                dve.sem_inc(s_tick)
                rows = lambda t: res[:, bass.ds(b0 + t * D, D)]
                statistics(rows, s_ln, base + 1)
                normalise(m * 2 + 1, rows, s_ln, base + 1, s_ln)
                dve.wait_ge(s_ln, base + 5)
                for t in range(JT):
                    ins = nc.vector.tensor_scalar(hs_hi[:, bass.ds(b0 + t * D, D)],
                                                  res[:, bass.ds(b0 + t * D, D)],
                                                  dcur[:, t:t + 1], None, ALU.mult)
                ins.then_inc(s_ln, 1)
                dve.wait_ge(s_ln, base + 6)
                for t in range(JT):
                    ins = nc.vector.scalar_tensor_tensor(
                        out=hs_lo[:, bass.ds(b0 + t * D, D)], in0=res[:, bass.ds(b0 + t * D, D)],
                        scalar=dcur[:, t:t + 1], in1=hs_hi[:, bass.ds(b0 + t * D, D)].bitcast(F32),
                        op0=ALU.mult, op1=ALU.subtract)
                ins.then_inc(s_h, 1)

            ACC_STEPS = UPB + 1
            def block_turn(g):
                for u in range(UPB):
                    dve.wait_ge(s_raw[u % RAW_SLOTS],
                                g * (16 * UPB // RAW_SLOTS) + 16 * (u // RAW_SLOTS + 1))
                    if u == 0:
                        if not isinstance(g, int) or g > 0:
                            dve.wait_ge(s_acc, g * ACC_STEPS)
                        nc.vector.tensor_copy(rowacc[:, :], slot(u)).then_inc(s_acc, 1)
                    else:
                        dve.wait_ge(s_acc, g * ACC_STEPS + u)
                        nc.vector.tensor_tensor(rowacc[:, :], rowacc[:, :], slot(u), ALU.add)\
                          .then_inc(s_acc, 1)
                    if u == UPB - 1:
                        dve.wait_ge(s_acc, g * ACC_STEPS + UPB)
                        nc.vector.tensor_tensor(rowsum[:, :], rowacc[:, 0:BLOCK], rowacc[:, BLOCK:UNIT],
                                                ALU.add).then_inc(s_acc, 1)
                    low(g * UPB + u, u)
                    if isinstance(g, int) and g == 0:
                        continue
                    if u == 3:
                        degree_value(g - 1)
                    if u == 4:
                        degree(g - 1)
                    if u == 5:
                        make_h(g - 1)

            block_turn(0)
            with dve.Fori(0, TURNS) as turn:
                block_turn(turn * 2 + 1)
                block_turn(turn * 2 + 2)
            block_turn(NB - 1)

            def aggregate(i):
                dve.wait_ge(s_used, SPLIT_SLOTS + N1 + LAST[i] + 1)
                if i >= 2:
                    dve.wait_ge(s_z, i - 1)
                if i == 0:
                    nc.vector.tensor_copy(hid[0][:, :], ah2_bank[0][:, :]).then_inc(s_agg, 1)
                else:
                    dve.wait_ge(s_part, i + 1)
                    nc.vector.tensor_tensor(hid[i % 2][:, :], ah2_bank[i % 2][:, :], cols(part, i),
                                            ALU.add).then_inc(s_agg, 1)

            def result(i):
                return lambda t: res[:, i * BLOCK + t * D:i * BLOCK + (t + 1) * D]

            for m in range(STEPS2):
                if m < len(UNITS2):
                    n = N1 + m
                    dve.wait_ge(s_raw[n % RAW_SLOTS], 16 * (n // RAW_SLOTS + 1))
                    low(n, n)
                if m == 3:
                    degree_value(NB - 1)
                if m == 4:
                    degree(NB - 1)
                if m == 5:
                    make_h(NB - 1)
                for i in range(NB):
                    if LAST[i] + NORM_LAG == m:
                        normalise(2 * NB + i, result(i), s_ln2, LN2_STEPS * i + 1, s_fin)
                for i in range(NB):
                    if LAST[i] + AGG_LAG == m:
                        aggregate(i)
                    if LAST[i] + STATS_LAG == m:
                        dve.wait_ge(s_relu, i + 1)
                        o = (i % 2) * BLOCK
                        nc.vector.tensor_tensor(cols(res, i), rowacc[:, o:o + BLOCK], cols(res, i), ALU.add)\
                          .then_inc(s_ln2, 1)
                        dve.wait_ge(s_ln2, LN2_STEPS * i + 1)
                        statistics(result(i), s_ln2, LN2_STEPS * i + 1)

        @block.tensor
        def _(pe):
            pe.sem_inc(s_used, SPLIT_SLOTS)

            def product(acc, w_hi, w_lo, j, s, half, first, last, open_end=False):
                wc = slice(j * P, (j + 1) * P)
                ac = slice((s % SPLIT_SLOTS) * UNIT + half * BLOCK, (s % SPLIT_SLOTS) * UNIT + (half + 1) * BLOCK)
                nc.tensor.matmul(acc[:, :], w_hi[:, wc], a_hi[:, ac], start=first, stop=False,
                                 skip_group_check=open_end)
                nc.tensor.matmul(acc[:, :], w_hi[:, wc], a_lo[:, ac], start=False, stop=False,
                                 skip_group_check=open_end)
                return nc.tensor.matmul(acc[:, :], w_lo[:, wc], a_hi[:, ac], start=False, stop=last,
                                        skip_group_check=open_end)

            def degree(m):
                for t in range(JT):
                    mm = nc.tensor.matmul(mix_bank[:, t:t + 1], rowsum[:, t * P:(t + 1) * P], ones[:, :],
                                          start=True, stop=True)
                mm.then_inc(s_deg, 1)

            def layer(m, l):
                for br in range(2):
                    pe.wait_ge(s_hid, m * HID_STEPS + (2 * l + br + 1))
                    c = W_LAYER[br][l]
                    nc.tensor.matmul(mlp_bank[br][:, :], wts[:, c:c + D], hid[br][:, :],
                                     start=True, stop=True).then_inc(s_mlp, 1)

            def merge(m):
                pe.wait_ge(s_hid, (m + 1) * HID_STEPS)
                pe.wait_ge(s_dinv, 2 * m + 2)
                for t in range(JT):
                    for br in range(2):
                        mm = nc.tensor.matmul(mix_bank[:, t * D:(t + 1) * D], hid[br][:, t * P:(t + 1) * P],
                                              wts[:, W_MERGE[br]:W_MERGE[br] + D],
                                              start=(br == 0), stop=(br == 1))
                mm.then_inc(s_mix, 1)

            MLP_AT = {0: lambda m: degree(m), 1: lambda m: layer(m, 0), 2: lambda m: layer(m, 1),
                      3: lambda m: layer(m, 2), 4: lambda m: merge(m)}

            pe.wait_ge(s_ones, 1)
            pe.wait_ge(s_w, 64)
            def block_turn(g, par, h_ready):
                for u in range(UPB):
                    k, b = u // UPC, ORDER[u // UPC]
                    j0 = b * JT + (u % UPC) * UT
                    if u % UPC == 0:
                        pe.wait_ge(s_xp, 2 * k + 2)
                    pe.wait_ge(s_lo, g * UPB + (u + 1))

                    def products_h():
                        pe.wait_ge(s_h, b + 1)
                        if b == 0 and u % UPC == 0:
                            pe.wait_ge(s_part, g)
                        for half in range(UT):
                            product(ah_bank, hs_hi, hs_lo, j0 + half, u, half,
                                    b == 0 and u % UPC == 0 and half == 0,
                                    u % UPC == UPC - 1 and half == UT - 1, open_end=True)

                    if b < HB:
                        h_ready(b, products_h)
                    for half in range(UT):
                        for br in range(2):
                            mm = product(sum_bank[par][br], x_hi[br], x_lo[br], j0 + half, u, half,
                                         u == 0 and half == 0, u == UPB - 1 and half == UT - 1)
                        if half == UT - 1:
                            mm.then_inc(s_used, 1)
                        if u * UT + half in MLP_AT and not (isinstance(g, int) and g == 0):
                            MLP_AT[u * UT + half](g - 1)

            def in_turn(first):
                def h_ready(b, step):
                    least = (b - first) // 2
                    if least < 0:
                        step()
                    else:
                        with pe.If(turn > least):
                            step()
                return h_ready

            block_turn(0, 0, lambda b, step: None)
            with pe.Fori(0, TURNS) as turn:
                block_turn(turn * 2 + 1, 1, in_turn(1))
                block_turn(turn * 2 + 2, 0, in_turn(2))
            block_turn(NB - 1, 1, lambda b, step: step())

            def out_product(i):
                pe.wait_ge(s_agg, i + 1)
                if i >= 2:
                    pe.wait_ge(s_relu, i - 1)
                for t in range(JT):
                    mm = nc.tensor.matmul(z_bank[i % 2][:, t * D:(t + 1) * D], hid[i % 2][:, t * P:(t + 1) * P],
                                          wts[:, W_GCN:W_GCN + D], start=True, stop=True)
                mm.then_inc(s_z, 1)

            for m, (i, b, u) in enumerate(UNITS2):
                n = N1 + m
                j0 = b * JT + u * UT
                if m == FIRST[i]:
                    if i == 1:
                        pe.wait_ge(s_part, NB)
                    if i >= 2:
                        pe.wait_ge(s_agg, i - 1)
                pe.wait_ge(s_h, b + 1)
                pe.wait_ge(s_lo, n + 1)
                for half in range(UT):
                    mm = product(ah2_bank[i % 2], hs_hi, hs_lo, j0 + half, n, half,
                                 m == FIRST[i] and half == 0, m == LAST[i] and half == UT - 1)
                    if half == UT - 1:
                        mm.then_inc(s_used, 1)
                    if m * UT + half in MLP_AT:
                        MLP_AT[m * UT + half](NB - 1)
                for q in range(NB):
                    if LAST[q] + OUT_LAG == m:
                        out_product(q)
            for q in range(NB):
                if LAST[q] + OUT_LAG >= len(UNITS2):
                    out_product(q)


def kernel(x, adj, L0_gnn_x2, L0_gnn_eps1, L0_gnn_eps2, L0_gnn_W1, L0_gnn_b1, L0_gnn_W2, L0_gnn_b2,
           L0_gnn_Wm, L0_gnn_bm, L1_gnn_W):
    import numpy as np
    import concourse.bacc as bacc
    from concourse.bass_utils import run_bass_kernel_spmd

    def c(a):
        return np.ascontiguousarray(np.asarray(a))

    def by_tile(a):
        return c(np.asarray(a).reshape(NB, JT, P, D).transpose(0, 2, 1, 3).reshape(NB, P, BLOCK))

    a = np.asarray(adj).reshape(NB, BLOCK, NB, UPC, UT, P)[:, :, ORDER]
    units = c(a.transpose(0, 2, 3, 5, 4, 1).reshape(N1, P, UNIT))
    w1, w2, wm = np.asarray(L0_gnn_W1), np.asarray(L0_gnn_W2), np.asarray(L0_gnn_Wm)
    weights = c(np.concatenate([*(w.T for w in w1), *(w.T for w in w2), wm[:, :D].T, wm[:, D:].T,
                                np.asarray(L1_gnn_W)], axis=1))
    arrays = {
        "adj": units, "x1": by_tile(x), "x2": by_tile(L0_gnn_x2), "weights": weights,
        "biases": c(np.concatenate([np.asarray(L0_gnn_b1).T, np.asarray(L0_gnn_b2).T], axis=1)),
        "eps": c(np.concatenate([np.asarray(L0_gnn_eps1), np.asarray(L0_gnn_eps2)])[None, :]),
        "bm": c(np.asarray(L0_gnn_bm)[None, :]),
    }
    nc = bacc.Bacc("TRN2", target_bir_lowering=False, num_devices=1)
    args = [nc.dram_tensor(name, a.shape, F32, kind="ExternalInput").ap() for name, a in arrays.items()]
    args.append(nc.dram_tensor("out", (NB, P, BLOCK), F32, kind="ExternalOutput").ap())
    build(nc, *args)
    r = run_bass_kernel_spmd(nc, [arrays], core_ids=[0])
    out = r.results[0]["out"]
    return np.ascontiguousarray(out.reshape(NB, P, JT, D).transpose(0, 2, 1, 3).reshape(N, D))
```

```python
import concourse.bass as bass
from concourse import mybir

F32 = mybir.dt.float32
F32R = mybir.dt.float32r
ALU = mybir.AluOpType
ACT = mybir.ActivationFunctionType

P = 128
N = 4096
D = 128
BLOCK = 512
NB = N // BLOCK
JT = BLOCK // P
UT = 2
UNIT = UT * BLOCK
UPC = JT // UT
UPB = NB * UPC
LAYERS = 3
LN_EPS = 1e-5

EARLY = 2
ORDER = list(range(NB - 1, NB - 1 - EARLY, -1)) + list(range(NB - EARLY))
POS = {b: k for k, b in enumerate(ORDER)}
HB = NB - EARLY

RAW_SLOTS = 8
SPLIT_SLOTS = 4

SWEEP2 = [(i, [b for b in range(min(i, HB), NB)]) for i in range(NB)]
UNITS2 = [(i, b, u) for i, blocks in SWEEP2 for b in blocks for u in range(UPC)]
N1 = NB * UPB
FIRST = [min(m for m, x in enumerate(UNITS2) if x[0] == i) for i in range(NB)]
LAST = [max(m for m, x in enumerate(UNITS2) if x[0] == i) for i in range(NB)]
AGG_LAG, OUT_LAG, RELU_LAG, ADD_LAG, STATS_LAG, MOMENTS_LAG, ROOT_LAG, RSTD_LAG, NORM_LAG = \
    4, 4, 8, 9, 10, 11, 12, 13, 14
STEPS2 = len(UNITS2) + NORM_LAG + 1

PAIRS = NB // 2
SPLIT2 = [(pair, br) for pair in (3, 0, 1) for br in range(2)] + \
    [(None, s) for s in range(SPLIT_SLOTS)] + [(2, br) for br in range(2)]
SPLIT2_SLOTS = len(SPLIT2)
FREED_BY = [max(POS[2 * pair], POS[2 * pair + 1]) * UPC + UPC - 1 if pair is not None
            else UPB - SPLIT_SLOTS + s for pair, s in SPLIT2]
PRE = 6
PRE_AFTER = {FREED_BY[m] + SPLIT_SLOTS: [q for q in range(PRE) if FREED_BY[q] == FREED_BY[m]]
             for m in range(PRE)}
N7 = (NB - 1) * UPB
TAIL = []
for u in range(UPB):
    TAIL += [("turn", u)] + [("sweep2", m) for m in PRE_AFTER.get(u, [])]
TAIL += [("sweep2", m) for m in range(PRE, len(UNITS2))]
AT_TURN = {u: N7 + k for k, (kind, u) in enumerate(TAIL) if kind == "turn"}
AT_SWEEP2 = {m: N7 + k for k, (kind, m) in enumerate(TAIL) if kind == "sweep2"}

W_LAYER = [[(3 * br + l) * D for l in range(LAYERS)] for br in range(2)]
W_MERGE = [6 * D, 7 * D]
W_GCN = 8 * D
B_LAYER = [[3 * br + l for l in range(LAYERS)] for br in range(2)]

TURNS = (NB - 2) // 2
HID_STEPS = 2 * (LAYERS + 1)
MLP_STEPS = 2 * LAYERS


def build(nc, adj, x1, x2, weights, biases, eps, bm, out):
    from contextlib import ExitStack

    with ExitStack() as ctx:
        def sb(name, shape, dt=F32):
            return ctx.enter_context(nc.sbuf_tensor(name, shape, dt))

        def bank(name):
            return ctx.enter_context(nc.psum_tensor(name, [P, BLOCK], F32))

        def sem(name):
            return ctx.enter_context(nc.semaphore(name))

        x_hi = [sb(f"x{br}_hi", [P, NB * BLOCK], F32R) for br in range(2)]
        x_lo = [sb(f"x{br}_lo", [P, NB * BLOCK], F32R) for br in range(2)]
        hs_hi = sb("hs_hi", [P, NB * BLOCK], F32R)
        hs_lo = sb("hs_lo", [P, NB * BLOCK], F32R)
        res = sb("res", [P, NB * BLOCK])
        part = sb("part", [P, NB * BLOCK])
        raw = sb("raw", [P, RAW_SLOTS * UNIT])
        a_hi = sb("a_hi", [P, SPLIT_SLOTS * UNIT], F32R)
        a_lo = sb("a_lo", [P, SPLIT_SLOTS * UNIT], F32R)
        rowacc = sb("rowacc", [P, UNIT])
        rowsum = sb("rowsum", [P, BLOCK])
        hid = [sb(f"hid{br}", [P, BLOCK]) for br in range(2)]
        wts = sb("wts", [P, 9 * D])
        bias = sb("bias", [P, 6])
        gain = sb("gain", [P, 2])
        bm_all = sb("bm_all", [P, D])
        ones = sb("ones", [P, 1])
        dinv = sb("dinv", [P, NB * JT])
        stats = sb("stats", [P, JT * 6])
        meanvar = sb("meanvar", [P, JT * 2])
        rstd = sb("rstd", [P, JT])
        shift = sb("shift", [P, JT])
        root = sb("root", [P, 3 * JT])
        dcur = sb("dcur", [P, JT])

        sum_bank = [[bank(f"sum{par}{br}") for br in range(2)] for par in range(2)]
        ah_bank = bank("ah")
        mlp_bank = [bank(f"mlp{br}") for br in range(2)]
        mix_bank = bank("mix")
        ah2_bank = [sum_bank[0][0], ah_bank]
        z_bank = [sum_bank[0][1], sum_bank[1][1]]

        s_x = [sem(f"x_loaded{k}") for k in range(NB)]
        s_xh = sem("x_hi_ready")
        s_xp = sem("x_parts_ready")
        s_res = sem("x_plus_bm")
        s_w = sem("weights_loaded")
        s_ones = sem("ones_ready")
        s_gain = sem("gain_ready")
        s_raw = [sem(f"raw_loaded{s}") for s in range(RAW_SLOTS)]
        s_hi = sem("a_hi_ready")
        s_lo = sem("a_lo_ready")
        s_used = sem("split_slots_free")
        s_acc = sem("rowacc_step")
        s_hid = sem("hidden_ready")
        s_mlp = sem("layer_done")
        s_deg = sem("degree_done")
        s_dinv = sem("dinv_ready")
        s_mix = sem("mix_done")
        s_ln = sem("ln_step")
        s_h = sem("h_ready")
        s_part = sem("part_saved")
        s_agg = sem("agg_ready")
        s_z = sem("z_done")
        s_relu = sem("relu_ready")
        s_ln2 = sem("ln2_step")
        s_root = sem("root_step")
        s_tick = sem("vector_tick")
        s_shift = sem("shift_ready")
        s_sqrt = sem("sqrt_done")
        s_fin = sem("result_ready")
        s_out = sem("last_stored")
        s_out_pool = sem("others_stored")

        block = ctx.enter_context(nc.Block())

        LN_STEPS = 6
        LN2_STEPS = 4
        ROOT_STEPS = 4

        def slot(n):
            return raw[:, (n % RAW_SLOTS) * UNIT:(n % RAW_SLOTS + 1) * UNIT]

        def split(s):
            return a_hi, a_lo, slice((s % SPLIT_SLOTS) * UNIT, (s % SPLIT_SLOTS + 1) * UNIT)

        def split2(m):
            pair, s = SPLIT2[m % SPLIT2_SLOTS]
            if pair is None:
                return split(s)
            return x_hi[s], x_lo[s], slice(pair * UNIT, (pair + 1) * UNIT)

        def free2(m):
            if m < SPLIT2_SLOTS:
                return SPLIT_SLOTS + N7 + FREED_BY[m] + 1
            return SPLIT_SLOTS + N1 + m - SPLIT2_SLOTS + 1

        def loads(n):
            return 16 * (n // RAW_SLOTS + 1)

        def cols(t, b, n=1):
            return t[:, b * BLOCK:(b + n) * BLOCK]

        def stage(k):
            return cols(part, k)

        @block.sync
        def _(sp):
            def load_x(k):
                sp.dma_start(cols(res, ORDER[k]), x1[ORDER[k]]).then_inc(s_x[k], 16)
                sp.dma_start(stage(k), x2[ORDER[k]]).then_inc(s_x[k], 16)

            load_x(0)
            for n in range(UPB):
                if n >= RAW_SLOTS:
                    sp.wait_ge(s_lo, n - RAW_SLOTS + 1)
                sp.dma_start(slot(n), adj[n]).then_inc(s_raw[n % RAW_SLOTS], 16)
                if n == 0:
                    load_x(1)
                if n == 4:
                    sp.dma_start(wts[:, :], weights).then_inc(s_w, 16)
                if n % UPC == UPC - 1 and n // UPC + 2 < NB:
                    load_x(n // UPC + 2)
            with sp.Fori(UPB // RAW_SLOTS, N7 // RAW_SLOTS) as turn:
                for s in range(RAW_SLOTS):
                    n = turn * RAW_SLOTS + s
                    sp.wait_ge(s_lo, turn * RAW_SLOTS + (s - RAW_SLOTS + 1))
                    sp.dma_start(slot(s), adj[bass.ds(n, 1)].rearrange("a p f -> p (a f)"))\
                      .then_inc(s_raw[s], 16)
            for n, (kind, k) in enumerate(TAIL, N7):
                if kind == "turn":
                    source = N7 + k
                else:
                    i, b, u = UNITS2[k]
                    source = i * UPB + POS[b] * UPC + u
                sp.wait_ge(s_lo, n - RAW_SLOTS + 1)
                sp.dma_start(slot(n), adj[source]).then_inc(s_raw[n % RAW_SLOTS], 16)
            sp.wait_ge(s_fin, NB)
            sp.dma_start(out[NB - 1], cols(res, NB - 1)).then_inc(s_out, 16)
            sp.wait_ge(s_out, 16)

        @block.gpsimd
        def _(pool):
            pool.memset(ones[:, :], 1.0).then_inc(s_ones, 1)

            pool.wait_ge(s_w, 64)
            pool.wait_ge(s_xp, 2 * NB)
            for b in range(NB):
                r = cols(res, b).rearrange("p (t d) -> p t d", d=D)
                pool.tensor_tensor(r, r, bm_all[:, None, :].to_broadcast([P, JT, D]),
                                   ALU.add).then_inc(s_res, 1)

            for i in range(NB - 1):
                pool.wait_ge(s_fin, i + 1)
                pool.dma_start(out[i], cols(res, i)).then_inc(s_out_pool, 16)
            pool.wait_ge(s_out_pool, 16 * (NB - 1))

        @block.scalar
        def _(act):
            act.dma_start(bias[:, :], biases).then_inc(s_w, 16)
            act.dma_start(bm_all[:, :], bm.to_broadcast([P, D])).then_inc(s_w, 16)
            act.dma_start(gain[:, :], eps.to_broadcast([P, 2])).then_inc(s_w, 16)

            def high(s, loaded, free, to):
                hi, _, c = to
                act.wait_ge(s_raw[s % RAW_SLOTS], loaded)
                act.wait_ge(s_used, free)
                nc.scalar.activation(hi[:, c], slot(s), ACT.Copy).then_inc(s_hi, 1)

            def high2(m):
                high(AT_SWEEP2[m], loads(AT_SWEEP2[m]), free2(m), split2(m))

            def sums_out(m, par):
                act.wait_ge(s_used, (m + 1) * UPB + SPLIT_SLOTS)
                for br in range(2):
                    nc.scalar.activation(hid[br][:, :], sum_bank[par][br][:, :], ACT.Identity,
                                         scale=gain[:, br:br + 1]).then_inc(s_hid, 1)

            def relus(m, l):
                for br in range(2):
                    act.wait_ge(s_mlp, m * MLP_STEPS + (2 * l + br + 1))
                    c = B_LAYER[br][l]
                    nc.scalar.activation(hid[br][:, :], mlp_bank[br][:, :], ACT.Relu,
                                         bias=bias[:, c:c + 1]).then_inc(s_hid, 1)

            def save_part(m):
                nc.scalar.activation(part[:, bass.ds(m * BLOCK, BLOCK)], ah_bank[:, :],
                                     ACT.Copy).then_inc(s_part, 1)

            def x_high(q):
                k, br = q // 2, q % 2
                act.wait_ge(s_x[k], 32)
                nc.scalar.activation(cols(x_hi[br], ORDER[k]), cols(res, ORDER[k]) if br == 0 else stage(k),
                                     ACT.Copy).then_inc(s_xh, 1)

            def block_turn(g, par, has_part=lambda step: step(), last=False):
                for u in range(UPB):
                    if last:
                        high(AT_TURN[u], loads(AT_TURN[u]), g * UPB + u + 1, split(u))
                        for m in PRE_AFTER.get(u, []):
                            high2(m)
                    else:
                        high(u, g * loads(UPB - 1) + loads(u), g * UPB + (u + 1), split(u))
                    if isinstance(g, int) and g == 0 and u + 2 < 2 * NB:
                        x_high(u + 2)
                    if isinstance(g, int) and g == 0:
                        continue
                    if u == 2:
                        sums_out(g - 1, 1 - par)
                    if u == 3:
                        relus(g - 1, 0)
                        square_root((g - 1) * 2)
                    if u == 4:
                        relus(g - 1, 1)
                        relus(g - 1, 2)
                        has_part(lambda: save_part(g - 1))
                    if u == 6:
                        square_root((g - 1) * 2 + 1)

            def square_root(call):
                act.wait_ge(s_root, call * ROOT_STEPS + 1)
                nc.scalar.activation(root[:, JT:2 * JT], root[:, 0:JT], ACT.Sqrt).then_inc(s_sqrt, 1)

            def not_first(step):
                with act.If(turn > 0):
                    step()

            act.sem_inc(s_part, 1)
            x_high(0)
            x_high(1)
            block_turn(0, 0)
            act.wait_ge(s_gain, 1)
            with act.Fori(0, TURNS) as turn:
                block_turn(turn * 2 + 1, 1, not_first)
                block_turn(turn * 2 + 2, 0)
            block_turn(NB - 1, 1, last=True)
            for m in range(PRE, STEPS2):
                if m < len(UNITS2):
                    high2(m)
                if m == PRE + 2:
                    sums_out(NB - 1, 1)
                    save_part(NB - 1)
                if m == PRE + 3:
                    relus(NB - 1, 0)
                    square_root((NB - 1) * 2)
                if m == PRE + 4:
                    relus(NB - 1, 1)
                    relus(NB - 1, 2)
                if m == PRE + 8:
                    square_root((NB - 1) * 2 + 1)
                for i in range(NB):
                    if LAST[i] + RELU_LAG == m:
                        act.wait_ge(s_z, i + 1)
                        if i >= 2:
                            act.wait_ge(s_ln2, LN2_STEPS * (i - 2) + 1)
                        for t in range(JT):
                            o = (i % 2) * BLOCK + t * P
                            c = i * JT + t
                            ins = nc.scalar.activation(rowacc[:, o:o + D], z_bank[i % 2][:, t * D:(t + 1) * D],
                                                       ACT.Relu, scale=dinv[:, c:c + 1])
                        ins.then_inc(s_relu, 1)
                    if LAST[i] + ROOT_LAG == m:
                        square_root(2 * NB + i)
                    if LAST[i] + NORM_LAG == m:
                        act.wait_ge(s_shift, i + 1)
                        for t in range(JT):
                            r = res[:, i * BLOCK + t * D:i * BLOCK + (t + 1) * D]
                            ins = nc.scalar.activation(r, r, ACT.Identity, bias=shift[:, t:t + 1],
                                                       scale=rstd[:, t:t + 1])
                        ins.then_inc(s_fin, 1)

        @block.vector
        def _(dve):
            def x_low(q):
                k, br = q // 2, q % 2
                dve.wait_ge(s_xh, q + 1)
                nc.vector.tensor_tensor(cols(x_lo[br], ORDER[k]), cols(res, ORDER[k]) if br == 0 else stage(k),
                                        cols(x_hi[br], ORDER[k]).bitcast(F32), ALU.subtract).then_inc(s_xp, 1)

            def low(n, s, to):
                hi, lo, c = to
                dve.wait_ge(s_hi, n + 1)
                nc.vector.tensor_tensor(lo[:, c], slot(s), hi[:, c].bitcast(F32),
                                        ALU.subtract).then_inc(s_lo, 1)

            def low2(m):
                n = AT_SWEEP2[m]
                dve.wait_ge(s_raw[n % RAW_SLOTS], loads(n))
                low(n, n, split2(m))

            value, sroot, fix = root[:, 0:JT], root[:, JT:2 * JT], root[:, 2 * JT:3 * JT]

            def invert(call, r):
                base = call * ROOT_STEPS + 1
                dve.wait_ge(s_sqrt, call + 1)
                nc.vector.reciprocal(r, sroot).then_inc(s_root, 1)
                dve.wait_ge(s_root, base + 1)
                nc.vector.tensor_tensor(fix, r, r, ALU.mult).then_inc(s_root, 1)

            def newton(call, r, done):
                base = call * ROOT_STEPS + 1
                dve.wait_ge(s_root, base + 2)
                nc.vector.scalar_tensor_tensor(out=fix, in0=fix, scalar=-0.5, in1=value,
                                               op0=ALU.mult, op1=ALU.mult).then_inc(s_root, 1)
                dve.wait_ge(s_root, base + 3)
                nc.vector.scalar_tensor_tensor(out=r, in0=fix, scalar=1.5, in1=r,
                                               op0=ALU.add, op1=ALU.mult).then_inc(done, 1)

            def degree_value(m):
                dve.wait_ge(s_deg, m + 1)
                nc.vector.tensor_copy(value, mix_bank[:, 0:JT]).then_inc(s_root, 1)

            def degree(m):
                invert(m * 2, dcur[:, :])
                newton(m * 2, dcur[:, :], s_dinv)
                dve.wait_ge(s_dinv, 2 * m + 1)
                nc.vector.tensor_copy(dinv[:, bass.ds(m * JT, JT)], dcur[:, :]).then_inc(s_dinv, 1)

            def statistics(r, s, base):
                dve.wait_ge(s, base + 1)
                dve.sem_inc(s_tick)
                for t in range(JT):
                    ins = nc.vector.bn_stats(stats[:, 6 * t:6 * t + 6], r(t))
                ins.then_inc(s, 1)

            def moments(s, base):
                dve.wait_ge(s, base + 2)
                dve.sem_inc(s_tick)
                for t in range(JT):
                    ins = nc.vector.bn_aggr(meanvar[:, 2 * t:2 * t + 2], stats[:, 6 * t:6 * t + 6])
                ins.then_inc(s, 1)
                dve.wait_ge(s, base + 3)
                nc.vector.tensor_scalar(value, meanvar[:, 1:2 * JT:2], LN_EPS, None, ALU.add)\
                  .then_inc(s_root, 1)

            def h_rows(m):
                return lambda t: res[:, bass.ds(m * BLOCK + t * D, D)]

            def h_add(m):
                dve.wait_ge(s_mix, m + 1)
                dve.wait_ge(s_res, NB)
                r = res[:, bass.ds(m * BLOCK, BLOCK)]
                nc.vector.tensor_tensor(r, mix_bank[:, :], r, ALU.add).then_inc(s_ln, 1)

            def h_normalise(m):
                r = h_rows(m)
                dve.wait_ge(s_ln, m * LN_STEPS + 4)
                for t in range(JT):
                    ins = nc.vector.tensor_scalar(r(t), r(t), meanvar[:, 2 * t:2 * t + 1],
                                                  rstd[:, t:t + 1], ALU.subtract, ALU.mult)
                ins.then_inc(s_ln, 1)

            def h_high(m):
                r = h_rows(m)
                dve.wait_ge(s_ln, m * LN_STEPS + 5)
                for t in range(JT):
                    ins = nc.vector.tensor_scalar(hs_hi[:, bass.ds(m * BLOCK + t * D, D)], r(t),
                                                  dcur[:, t:t + 1], None, ALU.mult)
                ins.then_inc(s_ln, 1)

            def h_low(m):
                r = h_rows(m)
                dve.wait_ge(s_ln, m * LN_STEPS + 6)
                for t in range(JT):
                    c = bass.ds(m * BLOCK + t * D, D)
                    ins = nc.vector.scalar_tensor_tensor(
                        out=hs_lo[:, c], in0=r(t), scalar=dcur[:, t:t + 1], in1=hs_hi[:, c].bitcast(F32),
                        op0=ALU.mult, op1=ALU.subtract)
                ins.then_inc(s_h, 1)

            def make_h(m):
                base = m * LN_STEPS
                h_add(m)
                statistics(h_rows(m), s_ln, base)
                moments(s_ln, base)
                invert(m * 2 + 1, rstd[:, :])
                newton(m * 2 + 1, rstd[:, :], s_ln)
                h_normalise(m)
                h_high(m)
                h_low(m)

            ACC_STEPS = UPB + 1
            def block_turn(g, last=False):
                for u in range(UPB):
                    n = AT_TURN[u] if last else g * UPB + u
                    s = n if last else u
                    dve.wait_ge(s_raw[s % RAW_SLOTS], loads(s) if last else g * loads(UPB - 1) + loads(u))
                    if u == 0:
                        if not isinstance(g, int) or g > 0:
                            dve.wait_ge(s_acc, g * ACC_STEPS)
                        nc.vector.tensor_copy(rowacc[:, :], slot(s)).then_inc(s_acc, 1)
                    else:
                        dve.wait_ge(s_acc, g * ACC_STEPS + u)
                        nc.vector.tensor_tensor(rowacc[:, :], rowacc[:, :], slot(s), ALU.add)\
                          .then_inc(s_acc, 1)
                    if u == UPB - 1:
                        dve.wait_ge(s_acc, g * ACC_STEPS + UPB)
                        nc.vector.tensor_tensor(rowsum[:, :], rowacc[:, 0:BLOCK], rowacc[:, BLOCK:UNIT],
                                                ALU.add).then_inc(s_acc, 1)
                    low(n, s, split(u))
                    if last:
                        for m in PRE_AFTER.get(u, []):
                            low2(m)
                    if isinstance(g, int) and g == 0:
                        if u + 2 < 2 * NB:
                            x_low(u + 2)
                        continue
                    if u == 3:
                        degree_value(g - 1)
                    if u == 4:
                        degree(g - 1)
                    if u == 5:
                        make_h(g - 1)

            x_low(0)
            x_low(1)
            block_turn(0)
            dve.wait_ge(s_w, 64)
            nc.vector.tensor_scalar(gain[:, :], gain[:, :], 1.0, 1.0, ALU.add, ALU.add).then_inc(s_gain, 1)
            with dve.Fori(0, TURNS) as turn:
                block_turn(turn * 2 + 1)
                block_turn(turn * 2 + 2)
            block_turn(NB - 1, last=True)

            def aggregate(i):
                dve.wait_ge(s_used, SPLIT_SLOTS + N1 + LAST[i] + 1)
                if i >= 2:
                    dve.wait_ge(s_z, i - 1)
                if i == 0:
                    nc.vector.tensor_copy(hid[0][:, :], ah2_bank[0][:, :]).then_inc(s_agg, 1)
                else:
                    dve.wait_ge(s_part, i + 1)
                    nc.vector.tensor_tensor(hid[i % 2][:, :], ah2_bank[i % 2][:, :], cols(part, i),
                                            ALU.add).then_inc(s_agg, 1)

            def result(i):
                return lambda t: res[:, i * BLOCK + t * D:i * BLOCK + (t + 1) * D]

            h = NB - 1
            for m in range(PRE, STEPS2):
                if m < len(UNITS2):
                    low2(m)
                if m == PRE + 3:
                    degree_value(NB - 1)
                if m == PRE + 4:
                    degree(NB - 1)
                if m == PRE + 5:
                    h_add(h)
                if m == PRE + 6:
                    statistics(h_rows(h), s_ln, h * LN_STEPS)
                if m == PRE + 7:
                    moments(s_ln, h * LN_STEPS)
                if m == PRE + 8:
                    invert(h * 2 + 1, rstd[:, :])
                if m == PRE + 9:
                    newton(h * 2 + 1, rstd[:, :], s_ln)
                if m == PRE + 10:
                    h_normalise(h)
                if m == PRE + 11:
                    h_high(h)
                if m == PRE + 12:
                    h_low(h)
                for i in range(NB):
                    base = LN2_STEPS * i
                    lag = m - LAST[i]
                    if lag == AGG_LAG:
                        aggregate(i)
                    if lag == ADD_LAG:
                        dve.wait_ge(s_relu, i + 1)
                        o = (i % 2) * BLOCK
                        nc.vector.tensor_tensor(cols(res, i), rowacc[:, o:o + BLOCK], cols(res, i), ALU.add)\
                          .then_inc(s_ln2, 1)
                    if lag == STATS_LAG:
                        statistics(result(i), s_ln2, base)
                    if lag == MOMENTS_LAG:
                        moments(s_ln2, base)
                    if lag == ROOT_LAG:
                        if i >= 1:
                            dve.wait_ge(s_fin, i)
                        invert(2 * NB + i, rstd[:, :])
                    if lag == RSTD_LAG:
                        newton(2 * NB + i, rstd[:, :], s_ln2)
                        dve.wait_ge(s_ln2, base + 4)
                        nc.vector.scalar_tensor_tensor(out=shift[:, :], in0=meanvar[:, 0:2 * JT:2], scalar=-1.0,
                                                       in1=rstd[:, :], op0=ALU.mult, op1=ALU.mult)\
                          .then_inc(s_shift, 1)

        @block.tensor
        def _(pe):
            pe.sem_inc(s_used, SPLIT_SLOTS)

            def product(acc, w_hi, w_lo, j, at, half, first, last, open_end=False):
                hi, lo, c = at
                wc = slice(j * P, (j + 1) * P)
                ac = slice(c.start + half * BLOCK, c.start + (half + 1) * BLOCK)
                nc.tensor.matmul(acc[:, :], w_hi[:, wc], hi[:, ac], start=first, stop=False,
                                 skip_group_check=open_end)
                nc.tensor.matmul(acc[:, :], w_hi[:, wc], lo[:, ac], start=False, stop=False,
                                 skip_group_check=open_end)
                return nc.tensor.matmul(acc[:, :], w_lo[:, wc], hi[:, ac], start=False, stop=last,
                                        skip_group_check=open_end)

            def degree(m):
                for t in range(JT):
                    mm = nc.tensor.matmul(mix_bank[:, t:t + 1], rowsum[:, t * P:(t + 1) * P], ones[:, :],
                                          start=True, stop=True)
                mm.then_inc(s_deg, 1)

            def layer(m, l):
                for br in range(2):
                    pe.wait_ge(s_hid, m * HID_STEPS + (2 * l + br + 1))
                    c = W_LAYER[br][l]
                    nc.tensor.matmul(mlp_bank[br][:, :], wts[:, c:c + D], hid[br][:, :],
                                     start=True, stop=True).then_inc(s_mlp, 1)

            def merge(m):
                pe.wait_ge(s_hid, (m + 1) * HID_STEPS)
                pe.wait_ge(s_dinv, 2 * m + 2)
                for t in range(JT):
                    for br in range(2):
                        mm = nc.tensor.matmul(mix_bank[:, t * D:(t + 1) * D], hid[br][:, t * P:(t + 1) * P],
                                              wts[:, W_MERGE[br]:W_MERGE[br] + D],
                                              start=(br == 0), stop=(br == 1))
                mm.then_inc(s_mix, 1)

            MLP_AT = {0: lambda m: degree(m), 1: lambda m: layer(m, 0), 2: lambda m: layer(m, 1),
                      3: lambda m: layer(m, 2), 4: lambda m: merge(m)}

            def block_turn(g, par, h_ready, last=False):
                for u in range(UPB):
                    k, b = u // UPC, ORDER[u // UPC]
                    j0 = b * JT + (u % UPC) * UT
                    if u % UPC == 0:
                        pe.wait_ge(s_xp, 2 * k + 2)
                    pe.wait_ge(s_lo, AT_TURN[u] + 1 if last else g * UPB + (u + 1))

                    def products_h():
                        pe.wait_ge(s_h, b + 1)
                        if b == 0 and u % UPC == 0:
                            pe.wait_ge(s_part, g)
                        for half in range(UT):
                            product(ah_bank, hs_hi, hs_lo, j0 + half, split(u), half,
                                    b == 0 and u % UPC == 0 and half == 0,
                                    u % UPC == UPC - 1 and half == UT - 1, open_end=True)

                    if b < HB:
                        h_ready(b, products_h)
                    for half in range(UT):
                        for br in range(2):
                            mm = product(sum_bank[par][br], x_hi[br], x_lo[br], j0 + half, split(u), half,
                                         u == 0 and half == 0, u == UPB - 1 and half == UT - 1)
                        if half == UT - 1:
                            mm.then_inc(s_used, 1)
                        if u * UT + half in MLP_AT and not (isinstance(g, int) and g == 0):
                            MLP_AT[u * UT + half](g - 1)

            def in_turn(first):
                def h_ready(b, step):
                    least = (b - first) // 2
                    if least < 0:
                        step()
                    else:
                        with pe.If(turn > least):
                            step()
                return h_ready

            block_turn(0, 0, lambda b, step: None)
            pe.wait_ge(s_ones, 1)
            pe.wait_ge(s_w, 64)
            with pe.Fori(0, TURNS) as turn:
                block_turn(turn * 2 + 1, 1, in_turn(1))
                block_turn(turn * 2 + 2, 0, in_turn(2))
            block_turn(NB - 1, 1, lambda b, step: step(), last=True)

            def out_product(i):
                pe.wait_ge(s_agg, i + 1)
                if i >= 2:
                    pe.wait_ge(s_relu, i - 1)
                for t in range(JT):
                    mm = nc.tensor.matmul(z_bank[i % 2][:, t * D:(t + 1) * D], hid[i % 2][:, t * P:(t + 1) * P],
                                          wts[:, W_GCN:W_GCN + D], start=True, stop=True)
                mm.then_inc(s_z, 1)

            for m, (i, b, u) in enumerate(UNITS2):
                j0 = b * JT + u * UT
                if m == FIRST[i]:
                    if i == 1:
                        pe.wait_ge(s_part, NB)
                    if i >= 2:
                        pe.wait_ge(s_agg, i - 1)
                pe.wait_ge(s_h, b + 1)
                pe.wait_ge(s_lo, AT_SWEEP2[m] + 1)
                for half in range(UT):
                    mm = product(ah2_bank[i % 2], hs_hi, hs_lo, j0 + half, split2(m), half,
                                 m == FIRST[i] and half == 0, m == LAST[i] and half == UT - 1)
                    if half == UT - 1:
                        mm.then_inc(s_used, 1)
                    if m * UT + half in MLP_AT:
                        MLP_AT[m * UT + half](NB - 1)
                for q in range(NB):
                    if LAST[q] + OUT_LAG == m:
                        out_product(q)
            for q in range(NB):
                if LAST[q] + OUT_LAG >= len(UNITS2):
                    out_product(q)


def kernel(x, adj, L0_gnn_x2, L0_gnn_eps1, L0_gnn_eps2, L0_gnn_W1, L0_gnn_b1, L0_gnn_W2, L0_gnn_b2,
           L0_gnn_Wm, L0_gnn_bm, L1_gnn_W):
    import numpy as np
    import concourse.bacc as bacc
    from concourse.bass_utils import run_bass_kernel_spmd

    def c(a):
        return np.ascontiguousarray(np.asarray(a))

    def by_tile(a):
        return c(np.asarray(a).reshape(NB, JT, P, D).transpose(0, 2, 1, 3).reshape(NB, P, BLOCK))

    a = np.asarray(adj).reshape(NB, BLOCK, NB, UPC, UT, P)[:, :, ORDER]
    units = c(a.transpose(0, 2, 3, 5, 4, 1).reshape(N1, P, UNIT))
    w1, w2, wm = np.asarray(L0_gnn_W1), np.asarray(L0_gnn_W2), np.asarray(L0_gnn_Wm)
    weights = c(np.concatenate([*(w.T for w in w1), *(w.T for w in w2), wm[:, :D].T, wm[:, D:].T,
                                np.asarray(L1_gnn_W)], axis=1))
    arrays = {
        "adj": units, "x1": by_tile(x), "x2": by_tile(L0_gnn_x2), "weights": weights,
        "biases": c(np.concatenate([np.asarray(L0_gnn_b1).T, np.asarray(L0_gnn_b2).T], axis=1)),
        "eps": c(np.concatenate([np.asarray(L0_gnn_eps1), np.asarray(L0_gnn_eps2)])[None, :]),
        "bm": c(np.asarray(L0_gnn_bm)[None, :]),
    }
    nc = bacc.Bacc("TRN2", target_bir_lowering=False, num_devices=1)
    args = [nc.dram_tensor(name, a.shape, F32, kind="ExternalInput").ap() for name, a in arrays.items()]
    args.append(nc.dram_tensor("out", (NB, P, BLOCK), F32, kind="ExternalOutput").ap())
    build(nc, *args)
    r = run_bass_kernel_spmd(nc, [arrays], core_ids=[0])
    out = r.results[0]["out"]
    return np.ascontiguousarray(out.reshape(NB, P, JT, D).transpose(0, 2, 1, 3).reshape(N, D))
```

```python
import concourse.bass as bass
from concourse import mybir

F32 = mybir.dt.float32
F32R = mybir.dt.float32r
ALU = mybir.AluOpType
ACT = mybir.ActivationFunctionType

P = 128
N = 4096
D = 128
BLOCK = 512
NB = N // BLOCK
JT = BLOCK // P
UT = 2
UNIT = UT * BLOCK
UPC = JT // UT
UPB = NB * UPC
LAYERS = 3
LN_EPS = 1e-5

EARLY = 2
ORDER = list(range(NB - 1, NB - 1 - EARLY, -1)) + list(range(NB - EARLY))
POS = {b: k for k, b in enumerate(ORDER)}
HB = NB - EARLY

RAW_SLOTS = 8
SPLIT_SLOTS = 4

SWEEP2 = [(i, [b for b in range(min(i, HB), NB)]) for i in range(NB)]
UNITS2 = [(i, b, u) for i, blocks in SWEEP2 for b in blocks for u in range(UPC)]
N1 = NB * UPB
FIRST = [min(m for m, x in enumerate(UNITS2) if x[0] == i) for i in range(NB)]
LAST = [max(m for m, x in enumerate(UNITS2) if x[0] == i) for i in range(NB)]
STEP_NAMES = ("aggregate", "out", "relu", "add", "stats", "moments", "sqrt", "root", "rstd", "norm")
LAGS = {i: (4, 4, 9, 11, 12, 13, 16, 17, 18, 22) for i in range(NB)}
LAGS[NB - 4] = (4, 4, 8, 10, 11, 12, 15, 16, 17, 18)
LAGS[NB - 3] = (4, 4, 7, 8, 9, 10, 11, 11, 12, 13)
LAGS[NB - 2] = (4, 4, 6, 7, 8, 9, 10, 11, 12, 13)
LAGS[NB - 1] = (1, 1, 3, 5, 6, 7, 8, 9, 10, 11)
STEP_AT = {i: {name: LAST[i] + lag for name, lag in zip(STEP_NAMES, LAGS[i])} for i in range(NB)}
STEPS2 = max(at["norm"] for at in STEP_AT.values()) + 1
assert all(STEP_AT[i]["rstd"] <= STEP_AT[i + 2]["add"] for i in range(NB - 2))
assert all(STEP_AT[i]["norm"] <= STEP_AT[i + 1]["norm"] for i in range(NB - 1))

PAIRS = NB // 2
SPLIT2 = [(pair, br) for pair in (3, 0, 1) for br in range(2)] + \
    [(None, s) for s in range(SPLIT_SLOTS)] + [(2, br) for br in range(2)]
SPLIT2_SLOTS = len(SPLIT2)
FREED_BY = [max(POS[2 * pair], POS[2 * pair + 1]) * UPC + UPC - 1 if pair is not None
            else UPB - SPLIT_SLOTS + s for pair, s in SPLIT2]
PRE = 6
PRE_AFTER = {FREED_BY[m] + SPLIT_SLOTS: [q for q in range(PRE) if FREED_BY[q] == FREED_BY[m]]
             for m in range(PRE)}
N7 = (NB - 1) * UPB
TAIL = []
for u in range(UPB):
    TAIL += [("turn", u)] + [("sweep2", m) for m in PRE_AFTER.get(u, [])]
TAIL += [("sweep2", m) for m in range(PRE, len(UNITS2))]
AT_TURN = {u: N7 + k for k, (kind, u) in enumerate(TAIL) if kind == "turn"}
AT_SWEEP2 = {m: N7 + k for k, (kind, m) in enumerate(TAIL) if kind == "sweep2"}

W_LAYER = [[(3 * br + l) * D for l in range(LAYERS)] for br in range(2)]
W_MERGE = [6 * D, 7 * D]
W_GCN = 8 * D
B_LAYER = [[3 * br + l for l in range(LAYERS)] for br in range(2)]

POOL_FROM = 2
WARM = 4

TURNS = (NB - 2) // 2
HID_STEPS = 2 * (LAYERS + 1)
MLP_STEPS = 2 * LAYERS


def build(nc, adj, x1, x2, weights, biases, eps, bm, out):
    from contextlib import ExitStack

    with ExitStack() as ctx:
        def sb(name, shape, dt=F32):
            return ctx.enter_context(nc.sbuf_tensor(name, shape, dt))

        def bank(name):
            return ctx.enter_context(nc.psum_tensor(name, [P, BLOCK], F32))

        def sem(name):
            return ctx.enter_context(nc.semaphore(name))

        x_hi = [sb(f"x{br}_hi", [P, NB * BLOCK], F32R) for br in range(2)]
        x_lo = [sb(f"x{br}_lo", [P, NB * BLOCK], F32R) for br in range(2)]
        hs_hi = sb("hs_hi", [P, NB * BLOCK], F32R)
        hs_lo = sb("hs_lo", [P, NB * BLOCK], F32R)
        res = sb("res", [P, NB * BLOCK])
        part = sb("part", [P, NB * BLOCK])
        raw = sb("raw", [P, RAW_SLOTS * UNIT])
        a_hi = sb("a_hi", [P, SPLIT_SLOTS * UNIT], F32R)
        a_lo = sb("a_lo", [P, SPLIT_SLOTS * UNIT], F32R)
        rowacc = sb("rowacc", [P, UNIT])
        rowsum = sb("rowsum", [P, BLOCK])
        hid = [sb(f"hid{br}", [P, BLOCK]) for br in range(2)]
        wts = sb("wts", [P, 9 * D])
        bias = sb("bias", [P, 6])
        gain = sb("gain", [P, 2])
        bm_all = sb("bm_all", [P, D])
        ones = sb("ones", [P, 1])
        dinv = sb("dinv", [P, NB * JT])
        stats = [sb(f"stats{q}", [P, JT * 6]) for q in range(2)]
        meanvar = [sb(f"meanvar{q}", [P, JT * 2]) for q in range(2)]
        rstd = [sb(f"rstd{q}", [P, JT]) for q in range(2)]
        shift = [sb(f"shift{q}", [P, JT]) for q in range(2)]
        root = [sb(f"root{q}", [P, 3 * JT]) for q in range(2)]
        dcur = sb("dcur", [P, JT])

        sum_bank = [[bank(f"sum{par}{br}") for br in range(2)] for par in range(2)]
        ah_bank = bank("ah")
        mlp_bank = [bank(f"mlp{br}") for br in range(2)]
        mix_bank = bank("mix")
        ah2_bank = [sum_bank[0][0], ah_bank]
        z_bank = [sum_bank[0][1], sum_bank[1][1]]

        s_x = [sem(f"x_loaded{k}") for k in range(NB)]
        s_xh = sem("x_hi_ready")
        s_xp = sem("x_parts_ready")
        s_xp_pool = sem("x_parts_ready_pool")
        s_res = sem("x_plus_bm")
        s_w = sem("weights_loaded")
        s_ones = sem("ones_ready")
        s_gain = sem("gain_ready")
        s_raw = [sem(f"raw_loaded{s}") for s in range(RAW_SLOTS)]
        s_hi = sem("a_hi_ready")
        s_lo = sem("a_lo_ready")
        s_used = sem("split_slots_free")
        s_acc = sem("rowacc_step")
        s_hid = sem("hidden_ready")
        s_mlp = sem("layer_done")
        s_deg = sem("degree_done")
        s_dinv = sem("dinv_ready")
        s_mix = sem("mix_done")
        s_ln = sem("ln_step")
        s_h = sem("h_ready")
        s_part = sem("part_saved")
        s_agg = sem("agg_ready")
        s_z = sem("z_done")
        s_relu = sem("relu_ready")
        s_ln2 = [sem(f"ln2_step{q}") for q in range(2)]
        s_root = [sem(f"root_step{q}") for q in range(2)]
        s_tick = sem("vector_tick")
        s_shift = sem("shift_ready")
        s_sqrt = [sem(f"sqrt_done{q}") for q in range(2)]
        s_fin = sem("result_ready")
        s_out = sem("last_stored")
        s_out_pool = sem("others_stored")

        block = ctx.enter_context(nc.Block())

        LN_STEPS = 6
        LN2_STEPS = 4
        ROOT_STEPS = 4

        def end_root(i):
            return (2 * NB, 0)[i % 2] + i // 2, i % 2

        def slot(n):
            return raw[:, (n % RAW_SLOTS) * UNIT:(n % RAW_SLOTS + 1) * UNIT]

        def split(s):
            return a_hi, a_lo, slice((s % SPLIT_SLOTS) * UNIT, (s % SPLIT_SLOTS + 1) * UNIT)

        def split2(m):
            pair, s = SPLIT2[m % SPLIT2_SLOTS]
            if pair is None:
                return split(s)
            return x_hi[s], x_lo[s], slice(pair * UNIT, (pair + 1) * UNIT)

        def free2(m):
            if m < SPLIT2_SLOTS:
                return SPLIT_SLOTS + N7 + FREED_BY[m] + 1
            return SPLIT_SLOTS + N1 + m - SPLIT2_SLOTS + 1

        def loads(n):
            return 16 * (n // RAW_SLOTS + 1)

        def cols(t, b, n=1):
            return t[:, b * BLOCK:(b + n) * BLOCK]

        def stage(k):
            return cols(part, k)

        @block.sync
        def _(sp):
            def load_x(k):
                sp.dma_start(cols(res, ORDER[k]), x1[ORDER[k]]).then_inc(s_x[k], 16)
                sp.dma_start(stage(k), x2[ORDER[k]]).then_inc(s_x[k], 16)

            load_x(0)
            for n in range(UPB):
                if n >= RAW_SLOTS:
                    sp.wait_ge(s_lo, n - RAW_SLOTS + 1)
                sp.dma_start(slot(n), adj[n]).then_inc(s_raw[n % RAW_SLOTS], 16)
                if n == 0:
                    load_x(1)
                if n == 4:
                    sp.dma_start(wts[:, :], weights).then_inc(s_w, 16)
                if n % UPC == UPC - 1 and n // UPC + 2 < NB:
                    load_x(n // UPC + 2)
            with sp.Fori(UPB // RAW_SLOTS, N7 // RAW_SLOTS) as turn:
                for s in range(RAW_SLOTS):
                    n = turn * RAW_SLOTS + s
                    sp.wait_ge(s_lo, turn * RAW_SLOTS + (s - RAW_SLOTS + 1))
                    sp.dma_start(slot(s), adj[bass.ds(n, 1)].rearrange("a p f -> p (a f)"))\
                      .then_inc(s_raw[s], 16)
            for n, (kind, k) in enumerate(TAIL, N7):
                if kind == "turn":
                    source = N7 + k
                else:
                    i, b, u = UNITS2[k]
                    source = i * UPB + POS[b] * UPC + u
                sp.wait_ge(s_lo, n - RAW_SLOTS + 1)
                sp.dma_start(slot(n), adj[source]).then_inc(s_raw[n % RAW_SLOTS], 16)
            sp.wait_ge(s_fin, NB)
            sp.dma_start(out[NB - 1], cols(res, NB - 1)).then_inc(s_out, 16)
            sp.wait_ge(s_out, 16)

        @block.gpsimd
        def _(pool):
            pool.memset(ones[:, :], 1.0)
            pool.memset(hid[0][:, :], 0.0).then_inc(s_ones, 1)

            for k in range(POOL_FROM, NB):
                pool.wait_ge(s_xh, 2 * k + 2)
                c = slice(ORDER[k] * BLOCK, (ORDER[k] + 1) * BLOCK)
                pool.tensor_tensor(x_lo[1][:, c], stage(k), x_hi[1][:, c].bitcast(F32),
                                   ALU.subtract).then_inc(s_xp_pool, 1)

            pool.wait_ge(s_w, 64)
            pool.wait_ge(s_xp, NB + POOL_FROM)
            for b in range(NB):
                r = cols(res, b).rearrange("p (t d) -> p t d", d=D)
                pool.tensor_tensor(r, r, bm_all[:, None, :].to_broadcast([P, JT, D]),
                                   ALU.add).then_inc(s_res, 1)

            for i in range(NB - 1):
                pool.wait_ge(s_fin, i + 1)
                pool.dma_start(out[i], cols(res, i)).then_inc(s_out_pool, 16)
            pool.wait_ge(s_out_pool, 16 * (NB - 1))

        @block.scalar
        def _(act):
            act.dma_start(bias[:, :], biases).then_inc(s_w, 16)
            act.dma_start(bm_all[:, :], bm.to_broadcast([P, D])).then_inc(s_w, 16)
            act.dma_start(gain[:, :], eps.to_broadcast([P, 2])).then_inc(s_w, 16)

            def high(s, loaded, free, to):
                hi, _, c = to
                act.wait_ge(s_raw[s % RAW_SLOTS], loaded)
                act.wait_ge(s_used, free)
                nc.scalar.activation(hi[:, c], slot(s), ACT.Copy).then_inc(s_hi, 1)

            def high2(m):
                high(AT_SWEEP2[m], loads(AT_SWEEP2[m]), free2(m), split2(m))

            def sums_out(m, par):
                act.wait_ge(s_used, (m + 1) * UPB + SPLIT_SLOTS)
                for br in range(2):
                    nc.scalar.activation(hid[br][:, :], sum_bank[par][br][:, :], ACT.Identity,
                                         scale=gain[:, br:br + 1]).then_inc(s_hid, 1)

            def relus(m, l):
                for br in range(2):
                    act.wait_ge(s_mlp, m * MLP_STEPS + (2 * l + br + 1))
                    c = B_LAYER[br][l]
                    nc.scalar.activation(hid[br][:, :], mlp_bank[br][:, :], ACT.Relu,
                                         bias=bias[:, c:c + 1]).then_inc(s_hid, 1)

            def save_part(m):
                nc.scalar.activation(part[:, bass.ds(m * BLOCK, BLOCK)], ah_bank[:, :],
                                     ACT.Copy).then_inc(s_part, 1)

            def x_high(q):
                k, br = q // 2, q % 2
                act.wait_ge(s_x[k], 32)
                nc.scalar.activation(cols(x_hi[br], ORDER[k]), cols(res, ORDER[k]) if br == 0 else stage(k),
                                     ACT.Copy).then_inc(s_xh, 1)

            def block_turn(g, par, has_part=lambda step: step(), last=False):
                for u in range(UPB):
                    if last:
                        high(AT_TURN[u], loads(AT_TURN[u]), g * UPB + u + 1, split(u))
                        for m in PRE_AFTER.get(u, []):
                            high2(m)
                    else:
                        high(u, g * loads(UPB - 1) + loads(u), g * UPB + (u + 1), split(u))
                    if isinstance(g, int) and g == 0 and u + 2 < 2 * NB:
                        x_high(u + 2)
                    if isinstance(g, int) and g == 0:
                        continue
                    if u == 2:
                        sums_out(g - 1, 1 - par)
                    if u == 3:
                        relus(g - 1, 0)
                        square_root((g - 1) * 2)
                    if u == 4:
                        relus(g - 1, 1)
                        relus(g - 1, 2)
                        has_part(lambda: save_part(g - 1))
                    if u == 6:
                        square_root((g - 1) * 2 + 1)

            def square_root(call, q=0):
                act.wait_ge(s_root[q], call * ROOT_STEPS + 1)
                nc.scalar.activation(root[q][:, JT:2 * JT], root[q][:, 0:JT], ACT.Sqrt).then_inc(s_sqrt[q], 1)

            def not_first(step):
                with act.If(turn > 0):
                    step()

            act.sem_inc(s_part, 1)
            x_high(0)
            x_high(1)
            block_turn(0, 0)
            act.wait_ge(s_gain, 1)
            with act.Fori(0, TURNS) as turn:
                block_turn(turn * 2 + 1, 1, not_first)
                block_turn(turn * 2 + 2, 0)
            block_turn(NB - 1, 1, last=True)
            for m in range(PRE, STEPS2):
                if m < len(UNITS2):
                    high2(m)
                if m == PRE + 2:
                    sums_out(NB - 1, 1)
                    save_part(NB - 1)
                if m == PRE + 3:
                    relus(NB - 1, 0)
                    square_root((NB - 1) * 2)
                if m == PRE + 4:
                    relus(NB - 1, 1)
                    relus(NB - 1, 2)
                if m == PRE + 8:
                    square_root((NB - 1) * 2 + 1)
                for i in range(NB):
                    at = STEP_AT[i]
                    if at["relu"] == m:
                        act.wait_ge(s_z, i + 1)
                        if i >= 2:
                            act.wait_ge(s_ln2[i % 2], LN2_STEPS * (i // 2 - 1) + 1)
                        for t in range(JT):
                            o = (i % 2) * BLOCK + t * P
                            c = i * JT + t
                            ins = nc.scalar.activation(rowacc[:, o:o + D], z_bank[i % 2][:, t * D:(t + 1) * D],
                                                       ACT.Relu, scale=dinv[:, c:c + 1])
                        ins.then_inc(s_relu, 1)
                    if at["sqrt"] == m:
                        square_root(*end_root(i))
                    if at["norm"] == m:
                        act.wait_ge(s_shift, i + 1)
                        for t in range(JT):
                            r = res[:, i * BLOCK + t * D:i * BLOCK + (t + 1) * D]
                            ins = nc.scalar.activation(r, r, ACT.Identity, bias=shift[i % 2][:, t:t + 1],
                                                       scale=rstd[i % 2][:, t:t + 1])
                        ins.then_inc(s_fin, 1)

        @block.vector
        def _(dve):
            def x_low(q):
                k, br = q // 2, q % 2
                dve.wait_ge(s_xh, q + 1)
                nc.vector.tensor_tensor(cols(x_lo[br], ORDER[k]), cols(res, ORDER[k]) if br == 0 else stage(k),
                                        cols(x_hi[br], ORDER[k]).bitcast(F32), ALU.subtract).then_inc(s_xp, 1)

            def low(n, s, to):
                hi, lo, c = to
                dve.wait_ge(s_hi, n + 1)
                nc.vector.tensor_tensor(lo[:, c], slot(s), hi[:, c].bitcast(F32),
                                        ALU.subtract).then_inc(s_lo, 1)

            def low2(m):
                n = AT_SWEEP2[m]
                dve.wait_ge(s_raw[n % RAW_SLOTS], loads(n))
                low(n, n, split2(m))

            value = [root[q][:, 0:JT] for q in range(2)]
            sroot = [root[q][:, JT:2 * JT] for q in range(2)]
            fix = [root[q][:, 2 * JT:3 * JT] for q in range(2)]

            def invert(r, call, q=0):
                base = call * ROOT_STEPS + 1
                dve.wait_ge(s_sqrt[q], call + 1)
                nc.vector.reciprocal(r, sroot[q]).then_inc(s_root[q], 1)
                dve.wait_ge(s_root[q], base + 1)
                nc.vector.tensor_tensor(fix[q], r, r, ALU.mult).then_inc(s_root[q], 1)

            def newton(r, done, call, q=0):
                base = call * ROOT_STEPS + 1
                dve.wait_ge(s_root[q], base + 2)
                nc.vector.scalar_tensor_tensor(out=fix[q], in0=fix[q], scalar=-0.5, in1=value[q],
                                               op0=ALU.mult, op1=ALU.mult).then_inc(s_root[q], 1)
                dve.wait_ge(s_root[q], base + 3)
                nc.vector.scalar_tensor_tensor(out=r, in0=fix[q], scalar=1.5, in1=r,
                                               op0=ALU.add, op1=ALU.mult).then_inc(done, 1)

            def degree_value(m):
                dve.wait_ge(s_deg, m + 1)
                nc.vector.tensor_copy(value[0], mix_bank[:, 0:JT]).then_inc(s_root[0], 1)

            def degree(m):
                invert(dcur[:, :], m * 2)
                newton(dcur[:, :], s_dinv, m * 2)
                dve.wait_ge(s_dinv, 2 * m + 1)
                nc.vector.tensor_copy(dinv[:, bass.ds(m * JT, JT)], dcur[:, :]).then_inc(s_dinv, 1)

            def statistics(r, s, base, q=0):
                dve.wait_ge(s, base + 1)
                dve.sem_inc(s_tick)
                for t in range(JT):
                    ins = nc.vector.bn_stats(stats[q][:, 6 * t:6 * t + 6], r(t))
                ins.then_inc(s, 1)

            def moments(s, base, q=0):
                dve.wait_ge(s, base + 2)
                dve.sem_inc(s_tick)
                for t in range(JT):
                    ins = nc.vector.bn_aggr(meanvar[q][:, 2 * t:2 * t + 2], stats[q][:, 6 * t:6 * t + 6])
                ins.then_inc(s, 1)
                dve.wait_ge(s, base + 3)
                nc.vector.tensor_scalar(value[q], meanvar[q][:, 1:2 * JT:2], LN_EPS, None, ALU.add)\
                  .then_inc(s_root[q], 1)

            def h_rows(m):
                return lambda t: res[:, bass.ds(m * BLOCK + t * D, D)]

            def h_add(m):
                dve.wait_ge(s_mix, m + 1)
                dve.wait_ge(s_res, NB)
                r = res[:, bass.ds(m * BLOCK, BLOCK)]
                nc.vector.tensor_tensor(r, mix_bank[:, :], r, ALU.add).then_inc(s_ln, 1)

            def h_normalise(m):
                r = h_rows(m)
                dve.wait_ge(s_ln, m * LN_STEPS + 4)
                for t in range(JT):
                    ins = nc.vector.tensor_scalar(r(t), r(t), meanvar[0][:, 2 * t:2 * t + 1],
                                                  rstd[0][:, t:t + 1], ALU.subtract, ALU.mult)
                ins.then_inc(s_ln, 1)

            def h_high(m):
                r = h_rows(m)
                dve.wait_ge(s_ln, m * LN_STEPS + 5)
                for t in range(JT):
                    ins = nc.vector.tensor_scalar(hs_hi[:, bass.ds(m * BLOCK + t * D, D)], r(t),
                                                  dcur[:, t:t + 1], None, ALU.mult)
                ins.then_inc(s_ln, 1)

            def h_low(m):
                r = h_rows(m)
                dve.wait_ge(s_ln, m * LN_STEPS + 6)
                for t in range(JT):
                    c = bass.ds(m * BLOCK + t * D, D)
                    ins = nc.vector.scalar_tensor_tensor(
                        out=hs_lo[:, c], in0=r(t), scalar=dcur[:, t:t + 1], in1=hs_hi[:, c].bitcast(F32),
                        op0=ALU.mult, op1=ALU.subtract)
                ins.then_inc(s_h, 1)

            def make_h(m):
                base = m * LN_STEPS
                h_add(m)
                statistics(h_rows(m), s_ln, base)
                moments(s_ln, base)
                invert(rstd[0][:, :], m * 2 + 1)
                newton(rstd[0][:, :], s_ln, m * 2 + 1)
                h_normalise(m)
                h_high(m)
                h_low(m)

            ACC_STEPS = UPB + 1
            def block_turn(g, last=False):
                for u in range(UPB):
                    n = AT_TURN[u] if last else g * UPB + u
                    s = n if last else u
                    dve.wait_ge(s_raw[s % RAW_SLOTS], loads(s) if last else g * loads(UPB - 1) + loads(u))
                    if u == 0:
                        if not isinstance(g, int) or g > 0:
                            dve.wait_ge(s_acc, g * ACC_STEPS)
                        nc.vector.tensor_copy(rowacc[:, :], slot(s)).then_inc(s_acc, 1)
                    else:
                        dve.wait_ge(s_acc, g * ACC_STEPS + u)
                        nc.vector.tensor_tensor(rowacc[:, :], rowacc[:, :], slot(s), ALU.add)\
                          .then_inc(s_acc, 1)
                    if u == UPB - 1:
                        dve.wait_ge(s_acc, g * ACC_STEPS + UPB)
                        nc.vector.tensor_tensor(rowsum[:, :], rowacc[:, 0:BLOCK], rowacc[:, BLOCK:UNIT],
                                                ALU.add).then_inc(s_acc, 1)
                    low(n, s, split(u))
                    if last:
                        for m in PRE_AFTER.get(u, []):
                            low2(m)
                    if isinstance(g, int) and g == 0 and u == UPB // 2:
                        dve.wait_ge(s_w, 64)
                        nc.vector.tensor_scalar(gain[:, :], gain[:, :], 1.0, 1.0, ALU.add, ALU.add)\
                          .then_inc(s_gain, 1)
                    if isinstance(g, int) and g == 0:
                        if u + 2 < 2 * NB and ((u + 2) % 2 == 0 or (u + 2) // 2 < POOL_FROM):
                            x_low(u + 2)
                        continue
                    if u == 3:
                        degree_value(g - 1)
                    if u == 4:
                        degree(g - 1)
                    if u == 5:
                        make_h(g - 1)

            x_low(0)
            x_low(1)
            block_turn(0)
            with dve.Fori(0, TURNS) as turn:
                block_turn(turn * 2 + 1)
                block_turn(turn * 2 + 2)
            block_turn(NB - 1, last=True)

            def aggregate(i):
                dve.wait_ge(s_used, SPLIT_SLOTS + N1 + LAST[i] + 1)
                if i >= 2:
                    dve.wait_ge(s_z, i - 1)
                if i == 0:
                    nc.vector.tensor_copy(hid[0][:, :], ah2_bank[0][:, :]).then_inc(s_agg, 1)
                else:
                    dve.wait_ge(s_part, i + 1)
                    nc.vector.tensor_tensor(hid[i % 2][:, :], ah2_bank[i % 2][:, :], cols(part, i),
                                            ALU.add).then_inc(s_agg, 1)

            def result(i):
                return lambda t: res[:, i * BLOCK + t * D:i * BLOCK + (t + 1) * D]

            h = NB - 1
            for m in range(PRE, STEPS2):
                if m < len(UNITS2):
                    low2(m)
                if m == PRE + 3:
                    degree_value(NB - 1)
                if m == PRE + 4:
                    degree(NB - 1)
                if m == PRE + 5:
                    h_add(h)
                if m == PRE + 6:
                    statistics(h_rows(h), s_ln, h * LN_STEPS)
                if m == PRE + 7:
                    moments(s_ln, h * LN_STEPS)
                if m == PRE + 8:
                    invert(rstd[0][:, :], h * 2 + 1)
                if m == PRE + 9:
                    newton(rstd[0][:, :], s_ln, h * 2 + 1)
                if m == PRE + 10:
                    h_normalise(h)
                if m == PRE + 11:
                    h_high(h)
                if m == PRE + 12:
                    h_low(h)
                for i in range(NB):
                    q, base = i % 2, LN2_STEPS * (i // 2)
                    at = STEP_AT[i]
                    if at["aggregate"] == m:
                        aggregate(i)
                    if at["add"] == m:
                        dve.wait_ge(s_relu, i + 1)
                        o = (i % 2) * BLOCK
                        nc.vector.tensor_tensor(cols(res, i), rowacc[:, o:o + BLOCK], cols(res, i), ALU.add)\
                          .then_inc(s_ln2[q], 1)
                    if at["stats"] == m:
                        statistics(result(i), s_ln2[q], base, q)
                    if at["moments"] == m:
                        moments(s_ln2[q], base, q)
                    if at["root"] == m:
                        if i >= 2:
                            dve.wait_ge(s_fin, i - 1)
                        invert(rstd[q][:, :], *end_root(i))
                    if at["rstd"] == m:
                        newton(rstd[q][:, :], s_ln2[q], *end_root(i))
                        dve.wait_ge(s_ln2[q], base + 4)
                        nc.vector.scalar_tensor_tensor(out=shift[q][:, :], in0=meanvar[q][:, 0:2 * JT:2], scalar=-1.0,
                                                       in1=rstd[q][:, :], op0=ALU.mult, op1=ALU.mult)\
                          .then_inc(s_shift, 1)

        @block.tensor
        def _(pe):
            pe.sem_inc(s_used, SPLIT_SLOTS)

            def product(acc, w_hi, w_lo, j, at, half, first, last, open_end=False):
                hi, lo, c = at
                wc = slice(j * P, (j + 1) * P)
                ac = slice(c.start + half * BLOCK, c.start + (half + 1) * BLOCK)
                nc.tensor.matmul(acc[:, :], w_hi[:, wc], hi[:, ac], start=first, stop=False,
                                 skip_group_check=open_end)
                nc.tensor.matmul(acc[:, :], w_hi[:, wc], lo[:, ac], start=False, stop=False,
                                 skip_group_check=open_end)
                return nc.tensor.matmul(acc[:, :], w_lo[:, wc], hi[:, ac], start=False, stop=last,
                                        skip_group_check=open_end)

            def degree(m):
                for t in range(JT):
                    mm = nc.tensor.matmul(mix_bank[:, t:t + 1], rowsum[:, t * P:(t + 1) * P], ones[:, :],
                                          start=True, stop=True)
                mm.then_inc(s_deg, 1)

            def layer(m, l):
                for br in range(2):
                    pe.wait_ge(s_hid, m * HID_STEPS + (2 * l + br + 1))
                    c = W_LAYER[br][l]
                    nc.tensor.matmul(mlp_bank[br][:, :], wts[:, c:c + D], hid[br][:, :],
                                     start=True, stop=True).then_inc(s_mlp, 1)

            def merge(m):
                pe.wait_ge(s_hid, (m + 1) * HID_STEPS)
                pe.wait_ge(s_dinv, 2 * m + 2)
                for t in range(JT):
                    for br in range(2):
                        mm = nc.tensor.matmul(mix_bank[:, t * D:(t + 1) * D], hid[br][:, t * P:(t + 1) * P],
                                              wts[:, W_MERGE[br]:W_MERGE[br] + D],
                                              start=(br == 0), stop=(br == 1))
                mm.then_inc(s_mix, 1)

            MLP_AT = {0: lambda m: degree(m), 1: lambda m: layer(m, 0), 2: lambda m: layer(m, 1),
                      3: lambda m: layer(m, 2), 4: lambda m: merge(m)}

            def block_turn(g, par, h_ready, last=False):
                for u in range(UPB):
                    k, b = u // UPC, ORDER[u // UPC]
                    j0 = b * JT + (u % UPC) * UT
                    if u % UPC == 0:
                        pe.wait_ge(s_xp, k + 1 + min(k + 1, POOL_FROM))
                        if k >= POOL_FROM:
                            pe.wait_ge(s_xp_pool, k + 1 - POOL_FROM)
                    pe.wait_ge(s_lo, AT_TURN[u] + 1 if last else g * UPB + (u + 1))

                    def products_h():
                        pe.wait_ge(s_h, b + 1)
                        if b == 0 and u % UPC == 0:
                            pe.wait_ge(s_part, g)
                        for half in range(UT):
                            product(ah_bank, hs_hi, hs_lo, j0 + half, split(u), half,
                                    b == 0 and u % UPC == 0 and half == 0,
                                    u % UPC == UPC - 1 and half == UT - 1, open_end=True)

                    for half in range(UT):
                        for br in range(2):
                            if b < HB and half == UT - 1 and br == 1:
                                h_ready(b, products_h)
                            mm = product(sum_bank[par][br], x_hi[br], x_lo[br], j0 + half, split(u), half,
                                         u == 0 and half == 0, u == UPB - 1 and half == UT - 1)
                        if half == UT - 1:
                            mm.then_inc(s_used, 1)
                        if u * UT + half in MLP_AT and not (isinstance(g, int) and g == 0):
                            MLP_AT[u * UT + half](g - 1)

            def in_turn(first):
                def h_ready(b, step):
                    least = (b - first) // 2
                    if least < 0:
                        step()
                    else:
                        with pe.If(turn > least):
                            step()
                return h_ready

            pe.wait_ge(s_ones, 1)
            for _ in range(WARM):
                nc.tensor.matmul(mix_bank[:, :], hid[0][:, 0:P], hid[0][:, :], start=True, stop=True)
            block_turn(0, 0, lambda b, step: None)
            pe.wait_ge(s_w, 64)
            with pe.Fori(0, TURNS) as turn:
                block_turn(turn * 2 + 1, 1, in_turn(1))
                block_turn(turn * 2 + 2, 0, in_turn(2))
            block_turn(NB - 1, 1, lambda b, step: step(), last=True)

            def out_product(i):
                pe.wait_ge(s_agg, i + 1)
                if i >= 2:
                    pe.wait_ge(s_relu, i - 1)
                for t in range(JT):
                    mm = nc.tensor.matmul(z_bank[i % 2][:, t * D:(t + 1) * D], hid[i % 2][:, t * P:(t + 1) * P],
                                          wts[:, W_GCN:W_GCN + D], start=True, stop=True)
                mm.then_inc(s_z, 1)

            for m, (i, b, u) in enumerate(UNITS2):
                j0 = b * JT + u * UT
                if m == FIRST[i]:
                    if i == 1:
                        pe.wait_ge(s_part, NB)
                    if i >= 2:
                        pe.wait_ge(s_agg, i - 1)
                pe.wait_ge(s_h, b + 1)
                pe.wait_ge(s_lo, AT_SWEEP2[m] + 1)
                for half in range(UT):
                    mm = product(ah2_bank[i % 2], hs_hi, hs_lo, j0 + half, split2(m), half,
                                 m == FIRST[i] and half == 0, m == LAST[i] and half == UT - 1)
                    if half == UT - 1:
                        mm.then_inc(s_used, 1)
                    if m * UT + half in MLP_AT:
                        MLP_AT[m * UT + half](NB - 1)
                for q in range(NB):
                    if STEP_AT[q]["out"] == m:
                        out_product(q)
            for q in range(NB):
                if STEP_AT[q]["out"] >= len(UNITS2):
                    out_product(q)


def kernel(x, adj, L0_gnn_x2, L0_gnn_eps1, L0_gnn_eps2, L0_gnn_W1, L0_gnn_b1, L0_gnn_W2, L0_gnn_b2,
           L0_gnn_Wm, L0_gnn_bm, L1_gnn_W):
    import numpy as np
    import concourse.bacc as bacc
    from concourse.bass_utils import run_bass_kernel_spmd

    def c(a):
        return np.ascontiguousarray(np.asarray(a))

    def by_tile(a):
        return c(np.asarray(a).reshape(NB, JT, P, D).transpose(0, 2, 1, 3).reshape(NB, P, BLOCK))

    a = np.asarray(adj).reshape(NB, BLOCK, NB, UPC, UT, P)[:, :, ORDER]
    units = c(a.transpose(0, 2, 3, 5, 4, 1).reshape(N1, P, UNIT))
    w1, w2, wm = np.asarray(L0_gnn_W1), np.asarray(L0_gnn_W2), np.asarray(L0_gnn_Wm)
    weights = c(np.concatenate([*(w.T for w in w1), *(w.T for w in w2), wm[:, :D].T, wm[:, D:].T,
                                np.asarray(L1_gnn_W)], axis=1))
    arrays = {
        "adj": units, "x1": by_tile(x), "x2": by_tile(L0_gnn_x2), "weights": weights,
        "biases": c(np.concatenate([np.asarray(L0_gnn_b1).T, np.asarray(L0_gnn_b2).T], axis=1)),
        "eps": c(np.concatenate([np.asarray(L0_gnn_eps1), np.asarray(L0_gnn_eps2)])[None, :]),
        "bm": c(np.asarray(L0_gnn_bm)[None, :]),
    }
    nc = bacc.Bacc("TRN2", target_bir_lowering=False, num_devices=1)
    args = [nc.dram_tensor(name, a.shape, F32, kind="ExternalInput").ap() for name, a in arrays.items()]
    args.append(nc.dram_tensor("out", (NB, P, BLOCK), F32, kind="ExternalOutput").ap())
    build(nc, *args)
    r = run_bass_kernel_spmd(nc, [arrays], core_ids=[0])
    out = r.results[0]["out"]
    return np.ascontiguousarray(out.reshape(NB, P, JT, D).transpose(0, 2, 1, 3).reshape(N, D))
```
